# Optimizing a Trainium2 kernel written in Bass

```python
import numpy as np
import jax
import jax.numpy as jnp

def _softmax(x, axis=-1):
    return jax.nn.softmax(x, axis=axis)

def _gelu(x):
    return jax.nn.gelu(x, approximate=True)

def _silu(x):
    return jax.nn.silu(x)

def _sigmoid(x):
    return jax.nn.sigmoid(x)

def _layernorm(x, axis=-1, eps=1e-05):
    m = jnp.mean(x, axis=axis, keepdims=True)
    v = jnp.var(x, axis=axis, keepdims=True)
    return (x - m) / jnp.sqrt(v + eps)

def _scatter_add(tgt, idx, src, axis=0):
    return tgt.at[idx].add(src)

def _segment_sum(src, seg, n):
    return jax.ops.segment_sum(src, seg, n)
kernel_name = 'mk_recurrent_d1_jaxref_r4_7b965c'

def setup_inputs(seed: int=0):
    np.random.seed(seed)
    _w = jnp.asarray

    def _L0_attn_setup():
        import jax, jax.numpy as jnp
        import numpy as np
        from jax import lax
        LN_EPS = 1e-05
        B, T, C = (4, 1024, 256)

        def _layernorm(x, w, b):
            mu = jnp.mean(x, axis=-1, keepdims=True)
            var = jnp.mean((x - mu) ** 2, axis=-1, keepdims=True)
            return (x - mu) * lax.rsqrt(var + LN_EPS) * w + b
        key = jax.random.key(seed)
        ks = jax.random.split(key, 12)
        s = 1.0 / np.sqrt(C)
        return {'x': jax.random.normal(ks[0], (B, T, C), dtype=jnp.float32), 'time_mix_k': jax.random.uniform(ks[1], (C,), dtype=jnp.float32), 'time_mix_v': jax.random.uniform(ks[2], (C,), dtype=jnp.float32), 'time_mix_r': jax.random.uniform(ks[3], (C,), dtype=jnp.float32), 'time_decay': jnp.zeros((C,), dtype=jnp.float32), 'time_first': jnp.zeros((C,), dtype=jnp.float32), 'Wk': jax.random.uniform(ks[4], (C, C), jnp.float32, -s, s), 'Wv': jax.random.uniform(ks[5], (C, C), jnp.float32, -s, s), 'Wr': jax.random.uniform(ks[6], (C, C), jnp.float32, -s, s), 'Wo': jax.random.uniform(ks[7], (C, C), jnp.float32, -s, s), 'ln_w': jnp.ones((C,), dtype=jnp.float32), 'ln_b': jnp.zeros((C,), dtype=jnp.float32)}
    _L0_attn_in = _L0_attn_setup()

    def _L0_ffn_setup():
        import jax, jax.numpy as jnp
        import numpy as np
        B, S, H = (2, 1024, 256)
        I = 128
        E = 8
        TOPK = 2
        NGROUP = 2
        TOPK_GROUP = 1
        ROUTED_SCALE = 1.0

        def _silu(x):
            return x * jax.nn.sigmoid(x)
        key = jax.random.key(seed)
        ks = jax.random.split(key, 9)

        def w(k, shape, s=0.05):
            return jax.random.normal(k, shape, dtype=jnp.float32) * s
        return {'hidden_states': jax.random.normal(ks[0], (B, S, H), dtype=jnp.float32), 'router_weight': w(ks[1], (E, H)), 'correction_bias': w(ks[2], (E,)), 'w_gate': w(ks[3], (E, H, I)), 'w_up': w(ks[4], (E, H, I)), 'w_down': w(ks[5], (E, I, H)), 'sw_gate': w(ks[6], (H, I)), 'sw_up': w(ks[7], (H, I)), 'sw_down': w(ks[8], (I, H))}
    _L0_ffn_in = _L0_ffn_setup()
    _d = {'L0_attn_x': _L0_attn_in['x'], 'L0_attn_time_mix_k': _L0_attn_in['time_mix_k'], 'L0_attn_time_mix_v': _L0_attn_in['time_mix_v'], 'L0_attn_time_mix_r': _L0_attn_in['time_mix_r'], 'L0_attn_time_decay': _L0_attn_in['time_decay'], 'L0_attn_time_first': _L0_attn_in['time_first'], 'L0_attn_Wk': _L0_attn_in['Wk'], 'L0_attn_Wv': _L0_attn_in['Wv'], 'L0_attn_Wr': _L0_attn_in['Wr'], 'L0_attn_Wo': _L0_attn_in['Wo'], 'L0_attn_ln_w': _L0_attn_in['ln_w'], 'L0_attn_ln_b': _L0_attn_in['ln_b'], 'L0_ffn_router_weight': _L0_ffn_in['router_weight'], 'L0_ffn_correction_bias': _L0_ffn_in['correction_bias'], 'L0_ffn_w_gate': _L0_ffn_in['w_gate'], 'L0_ffn_w_up': _L0_ffn_in['w_up'], 'L0_ffn_w_down': _L0_ffn_in['w_down'], 'L0_ffn_sw_gate': _L0_ffn_in['sw_gate'], 'L0_ffn_sw_up': _L0_ffn_in['sw_up'], 'L0_ffn_sw_down': _L0_ffn_in['sw_down']}
    _x0 = _d['L0_attn_x']
    _d['L0_attn_x'] = jax.random.normal(jax.random.fold_in(jax.random.key(seed), 1), (4, 1024, 256), dtype=_x0.dtype)
    del _x0
    return _d

def reference(L0_attn_x, L0_attn_time_mix_k, L0_attn_time_mix_v, L0_attn_time_mix_r, L0_attn_time_decay, L0_attn_time_first, L0_attn_Wk, L0_attn_Wv, L0_attn_Wr, L0_attn_Wo, L0_attn_ln_w, L0_attn_ln_b, L0_ffn_router_weight, L0_ffn_correction_bias, L0_ffn_w_gate, L0_ffn_w_up, L0_ffn_w_down, L0_ffn_sw_gate, L0_ffn_sw_up, L0_ffn_sw_down):

    def _L0_attn_ref(x, time_mix_k, time_mix_v, time_mix_r, time_decay, time_first, Wk, Wv, Wr, Wo, ln_w, ln_b):
        import jax, jax.numpy as jnp
        import numpy as np
        from jax import lax
        LN_EPS = 1e-05
        B, T, C = (4, 1024, 256)

        def _layernorm(x, w, b):
            mu = jnp.mean(x, axis=-1, keepdims=True)
            var = jnp.mean((x - mu) ** 2, axis=-1, keepdims=True)
            return (x - mu) * lax.rsqrt(var + LN_EPS) * w + b
        xt = _layernorm(x, ln_w, ln_b)
        x_prev = jnp.pad(xt[:, :-1], ((0, 0), (1, 0), (0, 0)))
        decay = jax.nn.sigmoid(time_decay)
        first = jnp.exp(time_first)
        mk, mv, mr = (time_mix_k, time_mix_v, time_mix_r)
        K = jnp.einsum('btc,dc->btd', xt * mk + x_prev * (1.0 - mk), Wk)
        V = jnp.einsum('btc,dc->btd', xt * mv + x_prev * (1.0 - mv), Wv)
        R = jax.nn.sigmoid(jnp.einsum('btc,dc->btd', xt * mr + x_prev * (1.0 - mr), Wr))

        def step(state, k_t):
            state = state * decay + k_t
            return (state, state)
        _, S = lax.scan(step, jnp.zeros((x.shape[0], K.shape[-1]), x.dtype), jnp.swapaxes(K, 0, 1))
        S = jnp.swapaxes(S, 0, 1)
        rwkv = (S * first + K) * V
        y = jnp.einsum('btc,dc->btd', R * rwkv, Wo)
        return x + y

    def _L0_ffn_ref(hidden_states, router_weight, correction_bias, w_gate, w_up, w_down, sw_gate, sw_up, sw_down):
        import jax, jax.numpy as jnp
        import numpy as np
        B, S, H = (2, 1024, 256)
        I = 128
        E = 8
        TOPK = 2
        NGROUP = 2
        TOPK_GROUP = 1
        ROUTED_SCALE = 1.0

        def _silu(x):
            return x * jax.nn.sigmoid(x)
        b, s, h = hidden_states.shape
        x = hidden_states.reshape(-1, h)
        logits = x @ router_weight.T
        scores = jax.nn.sigmoid(logits)
        scores_for_choice = scores + correction_bias[None, :]
        e_per_g = E // NGROUP
        group_scores = jax.lax.top_k(scores_for_choice.reshape(-1, NGROUP, e_per_g), 2)[0].sum(-1)
        group_idx = jax.lax.top_k(group_scores, TOPK_GROUP)[1]
        group_mask = jax.nn.one_hot(group_idx, NGROUP, dtype=scores.dtype).sum(1)
        score_mask = jnp.repeat(group_mask, e_per_g, axis=1)
        masked = jnp.where(score_mask > 0, scores_for_choice, 0.0)
        topk_idx = jax.lax.top_k(masked, TOPK)[1]
        topk_w = jnp.take_along_axis(scores, topk_idx, axis=1)
        topk_w = topk_w / (topk_w.sum(-1, keepdims=True) + 1e-20)
        topk_w = topk_w * ROUTED_SCALE
        comb = (jax.nn.one_hot(topk_idx, E, dtype=x.dtype) * topk_w[..., None]).sum(1)
        g = jnp.einsum('th,ehi->tei', x, w_gate)
        u = jnp.einsum('th,ehi->tei', x, w_up)
        y = jnp.einsum('tei,eih->teh', _silu(g) * u, w_down)
        routed = jnp.einsum('teh,te->th', y, comb).reshape(b, s, h)
        shared = _silu(hidden_states @ sw_gate) * (hidden_states @ sw_up) @ sw_down
        return routed + shared
    x = L0_attn_x
    xn = _layernorm(x, axis=-1)
    s = _L0_attn_ref(xn, L0_attn_time_mix_k, L0_attn_time_mix_v, L0_attn_time_mix_r, L0_attn_time_decay, L0_attn_time_first, L0_attn_Wk, L0_attn_Wv, L0_attn_Wr, L0_attn_Wo, L0_attn_ln_w, L0_attn_ln_b)
    g = _silu(_L0_ffn_ref(xn, L0_ffn_router_weight, L0_ffn_correction_bias, L0_ffn_w_gate, L0_ffn_w_up, L0_ffn_w_down, L0_ffn_sw_gate, L0_ffn_sw_up, L0_ffn_sw_down))
    x = x + s * g
    return x

_drawn_inputs = setup_inputs


def setup_inputs(seed=0):
    import zlib

    import numpy as np

    out = dict(_drawn_inputs(seed))
    spreads = {'L0_attn_time_decay': (0.0, 0.8),
     'L0_attn_time_first': (0.0, 0.8),
     'L0_attn_ln_w': (1.0, 0.6),
     'L0_attn_ln_b': (0.0, 0.8)}
    factors = {'L0_attn_time_mix_k': 6.686,
     'L0_attn_time_mix_v': 5.205,
     'L0_attn_time_mix_r': 8.0,
     'L0_attn_Wv': 2.67,
     'L0_attn_Wr': 8.0,
     'L0_attn_Wo': 2.674}
    for name, (base, spread) in spreads.items():
        noise = np.random.default_rng([zlib.crc32(name.encode()), seed]).standard_normal(out[name].shape)
        drawn = base * np.exp(spread * noise) if base else spread * noise
        out[name] = jnp.asarray(drawn.astype(out[name].dtype))
    for name, factor in factors.items():
        out[name] = (out[name] * factor).astype(out[name].dtype)
    return out
```

```python
from contextlib import ExitStack

import concourse.bass as bass
from concourse import mybir

F32 = mybir.dt.float32
F32R = mybir.dt.float32r
BF16 = mybir.dt.bfloat16
I32 = mybir.dt.int32
U32 = mybir.dt.uint32
ALU = mybir.AluOpType
ACT = mybir.ActivationFunctionType
AX = mybir.AxisListType
ds = bass.ds

P = 128
BATCH, SEQ, C = 4, 1024, 256
TOKENS = BATCH * SEQ
KC = C // P
EXPERTS, INNER, TOPK = 8, 128, 2
TILES = TOKENS // P
GROUP = 512
GT = GROUP // P
GROUPS = TOKENS // GROUP
ROW = C + 2
SORTED_TILES = TOKENS * TOPK // P + EXPERTS
SORTED_ROWS = SORTED_TILES * P
EW = 2 * KC * INNER + C
SHARED = EXPERTS
LN_EPS = 1e-5
OUT_OF_RANGE = float(TOKENS * TOPK)
REMOVED = -1e30
XRING, YRING = 8, 4


def half_tiles(s):
    return (s - 5) // 2 + 1

def run_steps(eng, step):
    for s in range(XRING):
        step(s, s, half_tiles(s), True)
    with eng.Fori(0, SORTED_TILES // XRING - 1) as k:
        for u in range(XRING):
            step(k * XRING + XRING + u, u + XRING, k * (XRING // 2) + half_tiles(u + XRING))
    for s in range(SORTED_TILES, SORTED_TILES + 3):
        step(s, s, half_tiles(s), True)


def gated_time_mix_kernel(nc, x, vectors, bias, router, attn_w, w_gate, w_up, w_down, out):
    sorted_rows = nc.dram_tensor("sorted_rows", [SORTED_ROWS, ROW], F32).ap()
    expert_rows = nc.dram_tensor("expert_rows", [TOKENS * TOPK, C], F32).ap()
    x_tiles = x.rearrange("b (j p) c -> p (b j) c", p=P)
    out_tiles = out.rearrange("b (j p) c -> p (b j) c", p=P)
    expert_tiles = expert_rows.rearrange("(j p k) c -> p j (k c)", p=P, k=TOPK)

    with ExitStack() as ctx:
        def sb(name, shape, dt=F32):
            return ctx.enter_context(nc.sbuf_tensor(name, shape, dt))

        def sem(name):
            return ctx.enter_context(nc.semaphore(name))

        rows = sb("rows", [P, TILES, ROW])
        shared_out = sb("shared_out", [P, TILES * C])
        wx_hi = sb("wx_hi", [P, EXPERTS + 1, EW], F32R)
        wx_lo = sb("wx_lo", [P, EXPERTS + 1, EW], F32R)
        wa_hi = sb("wa_hi", [P, 4, KC, C], F32R)
        wa_lo = sb("wa_lo", [P, 4, KC, C], F32R)
        wr_hi = sb("wr_hi", [P, KC, EXPERTS], F32R)
        wr_lo = sb("wr_lo", [P, KC, EXPERTS], F32R)
        in_hi = sb("in_hi", [P, 2, KC * GROUP], F32R)
        in_lo = sb("in_lo", [P, 2, KC * GROUP], F32R)
        mid_hi = sb("mid_hi", [P, 2, GROUP], F32R)
        mid_lo = sb("mid_lo", [P, 2, GROUP], F32R)

        xring = sb("xring", [P, XRING, ROW])
        yring = sb("yring", [P, YRING, C])
        dest = sb("dest", [P, XRING], U32)
        vec = sb("vec", [P, 7, KC])
        mk, mv, mr, v_decay, v_first, ln_w, ln_b = range(7)
        bias_sb = sb("bias_sb", [P, EXPERTS])
        router_f = sb("router_f", [P, KC, EXPERTS])
        decay = sb("decay", [P, KC])
        first = sb("first", [P, KC])
        stats = sb("stats", [P, TILES, 6])
        mean = sb("mean", [P, TILES])
        var = sb("var", [P, TILES])
        rstd = sb("rstd", [P, TILES])
        rstd2 = sb("rstd2", [P, TILES])
        tmp_a = sb("tmp_a", [P, TILES])
        tmp_b = sb("tmp_b", [P, TILES])
        ident = sb("ident", [P, P])
        before = sb("before", [P, P], BF16)
        ones = sb("ones", [P, P], BF16)
        place1 = sb("place1", [P, TILES], U32)
        place2 = sb("place2", [P, TILES], U32)
        weight1 = sb("weight1", [P, TILES])
        weight2 = sb("weight2", [P, TILES])
        my_place = sb("my_place", [P, SORTED_TILES])
        tile_no = sb("tile_no", [P, SORTED_TILES])
        weight_at = sb("weight_at", [P, SORTED_TILES], I32)
        int_tmp = sb("int_tmp", [P, SORTED_TILES], I32)
        last_s = sb("last_s", [P, KC])

        scratch = sb("scratch", [P, 8196])
        shared_end = TILES * C
        attn_stage = shared_out[:, shared_end - 4 * KC * C:shared_end].rearrange(
            "p (w k c) -> p w k c", w=4, k=KC)
        stage = scratch[:, 0:9 * EW].rearrange("p (e w) -> p e w", e=9)
        silu_g = scratch[:, 9 * EW:9 * EW + GROUP]
        h_shared = scratch[:, 9 * EW + GROUP:9 * EW + 2 * GROUP]
        GK = KC * GROUP
        z = scratch[:, 0:GK].rearrange("p (t c) -> p t c", t=GT)
        xt = [scratch[:, GK + h * KC * (GROUP + 1):GK + (h + 1) * KC * (GROUP + 1)].rearrange(
            "p (k t) -> p k t", k=KC) for h in range(2)]
        at = GK + 2 * KC * (GROUP + 1)
        diff = scratch[:, at:at + GK]
        mixed = scratch[:, at + GK:at + 2 * GK]
        s_state = scratch[:, at + 2 * GK:at + 3 * GK]
        rwkv = scratch[:, at + 3 * GK:at + 4 * GK]
        r_gate = scratch[:, at + 4 * GK:at + 5 * GK]
        ET = EXPERTS * TILES
        route_tmp = [scratch[:, at + n * ET:at + (n + 1) * ET] for n in range(16)]
        logit = scratch[:, 9 * EW + 2 * GROUP:9 * EW + 2 * GROUP + ET]
        silu_t = scratch[:, 7172:7172 + 2 * INNER].rearrange("p (b i) -> p b i", b=2)
        h_t = scratch[:, 7172 + 2 * INNER:7172 + 4 * INNER].rearrange("p (b i) -> p b i", b=2)
        y_pair = scratch[:, 0:4 * GK].rearrange("p (b t c) -> p b t c", b=2, t=GT)
        x_again = scratch[:, 4 * GK:6 * GK].rearrange("p (b t c) -> p b t c", b=2, t=GT)
        acc = scratch[:, 6 * GK:7 * GK].rearrange("p (t c) -> p t c", t=GT)
        x_norm = xring[:, :, 0:C]
        pad_row = yring[:, 0:2, :].rearrange("p a b -> p (a b)")[:, 0:ROW]

        bank = ctx.enter_context(nc.psum_tensor("bank", [P, 8, GROUP], F32))

        x_in = [sem(f"x_in{c}") for c in range(4)]
        rows_kept = sem("rows_kept")
        vec_in, router_in, shared_in = sem("vec_in"), sem("router_in"), sem("shared_in")
        attn_in, experts_in = sem("attn_in"), sem("experts_in")
        pads_out = sem("pads_out")
        scattered = [sem(f"scattered{g}") for g in range(GROUPS)]
        xring_in = [sem(f"xring_in{r}") for r in range(XRING)]
        yring_out = [sem(f"yring_out{r}") for r in range(YRING)]
        y_in = [sem(f"y_in{b}") for b in range(2)]
        out_out = [sem(f"out_out{b}") for b in range(2)]
        pad_set, const_set = sem("pad_set"), sem("const_set")
        attn_hi_set, experts_hi_set, expert_lo_set = sem("attn_hi_set"), sem("experts_hi_set"), sem("expert_lo_set")
        shared_w_set, params_set = sem("shared_w_set"), sem("params_set")
        dve_step = sem("dve_step")
        var_eps, root_set, norm_set = sem("var_eps"), sem("root_set"), sem("norm_set")
        rstd2_set = sem("rstd2_set")
        xn_set, t_done, thi_set, tlo_set = sem("xn_set"), sem("t_done"), sem("thi_set"), sem("tlo_set")
        gate_done, up_done, silu_set, h_set = sem("gate_done"), sem("up_done"), sem("silu_set"), sem("h_set")
        hhi_set, hlo_set, down_done, down_free = sem("hhi_set"), sem("hlo_set"), sem("down_done"), sem("down_free")
        logit_done, logit_read = sem("logit_done"), sem("logit_read")
        score_set, chosen_set, counted, places_set = sem("score_set"), sem("chosen_set"), sem("counted"), sem("places_set")
        rows_scattered = sem("rows_scattered")
        z_set, zt_done, xt_set, mixed_set = sem("z_set"), sem("zt_done"), sem("xt_set"), sem("mixed_set")
        mixhi_set, mixlo_set, k_done, v_done = sem("mixhi_set"), sem("mixlo_set"), sem("k_done"), sem("v_done")
        r_done, r_set, edge_set, diff_set = sem("r_done"), sem("r_set"), sem("edge_set"), sem("diff_set")
        scan_set, k_read, v_read, rwkv_set = sem("scan_set"), sem("k_read"), sem("v_read"), sem("rwkv_set")
        rwhi_set, rwlo_set, y_done, s_set = sem("rwhi_set"), sem("rwlo_set"), sem("y_done"), sem("s_set")
        e_t_done, e_hi_set, e_lo_set, e_gu_done = sem("e_t_done"), sem("e_hi_set"), sem("e_lo_set"), sem("e_gu_done")
        e_silu_set, e_h_set, e_ht_done = sem("e_silu_set"), sem("e_h_set"), sem("e_ht_done")
        e_hhi_set, e_hlo_set, e_down_done = sem("e_hhi_set"), sem("e_hlo_set"), sem("e_down_done")
        e_y_set = [sem("e_y_even_set"), sem("e_y_odd_set")]
        dest_set, scatter_ready = sem("dest_set"), sem("scatter_ready")
        part_set, routed_set, sum_set, silu_y_set = sem("part_set"), sem("routed_set"), sem("sum_set"), sem("silu_y_set")
        gated_set, out_set = sem("gated_set"), sem("out_set")

        block = ctx.enter_context(nc.Block())

        def f32(ap):
            return ap.bitcast(F32)

        @block.sync
        def _(sp):
            for c in range(4):
                n = TILES // 4
                sp.dma_start(rows[:, c * n:(c + 1) * n, 0:C], x_tiles[:, c * n:(c + 1) * n, :]).then_inc(x_in[c], 16)
            sp.wait_ge(pad_set, 3)
            sp.dma_start(sorted_rows.rearrange("(i p) c -> p i c", p=P),
                         pad_row.unsqueeze(1).to_broadcast([P, SORTED_TILES, ROW])).then_inc(pads_out, 16)

            sp.wait_ge(rows_scattered, GROUPS)

            def load_sorted(i, slot, reused):
                if reused:
                    sp.wait_ge(e_t_done, i - XRING + 1)
                    sp.wait_ge(dest_set, i - XRING + 1)
                sp.dma_start(xring[:, slot, :], sorted_rows[ds(i * P, P), :]).then_inc(xring_in[slot], 16)

            for r in range(XRING):
                load_sorted(r, r, False)
            with sp.Fori(0, SORTED_TILES // XRING - 1) as k:
                for r in range(XRING):
                    load_sorted(k * XRING + XRING + r, r, True)

            for n in range(YRING):
                sp.wait_ge(yring_out[n], 16 * (SORTED_TILES // YRING))

            def load_group(g, b, reused):
                if reused:
                    sp.wait_ge(out_set, g - 1)
                sp.dma_start(y_pair[:, b], expert_tiles[:, ds(g * GT, GT), :]).then_inc(y_in[b], 16)
                if reused:
                    sp.wait_ge(out_out[b], 8 * (g - b))
                sp.dma_start(x_again[:, b], x_tiles[:, ds(g * GT, GT), :]).then_inc(y_in[b], 16)

            def store_group(g, b):
                sp.wait_ge(out_set, g + 1)
                sp.dma_start(out_tiles[:, ds(g * GT, GT), :], x_again[:, b]).then_inc(out_out[b], 16)

            load_group(0, 0, False)
            load_group(1, 1, False)
            with sp.Fori(0, GROUPS // 2 - 1) as k:
                for b in range(2):
                    store_group(2 * k + b, b)
                    load_group(2 * k + 2 + b, b, True)
            for b in range(2):
                store_group(GROUPS - 2 + b, b)
            for b in range(2):
                sp.wait_ge(out_out[b], 16 * (GROUPS // 2))

        @block.gpsimd
        def _(pool):
            nc.gpsimd.memset(pad_row[:, 0:C], 0.0).then_inc(pad_set, 1)
            nc.gpsimd.memset(pad_row[:, C:C + 1], OUT_OF_RANGE).then_inc(pad_set, 1)
            nc.gpsimd.memset(pad_row[:, C + 1:C + 2], -1.0).then_inc(pad_set, 1)
            nc.gpsimd.memset(ident[:], 0.0).then_inc(const_set, 1)
            nc.gpsimd.memset(ones[:], 1.0).then_inc(const_set, 1)
            pool.wait_ge(const_set, 2)
            nc.gpsimd.affine_select(out=ident[:], in_=ident[:], compare_op=ALU.not_equal, fill=1.0, base=0,
                                    pattern=[[-1, P]], channel_multiplier=1).then_inc(const_set, 1)
            nc.gpsimd.affine_select(out=before[:], in_=ones[:], compare_op=ALU.is_gt, fill=0.0, base=0,
                                    pattern=[[1, P]], channel_multiplier=-1).then_inc(const_set, 1)
            nc.gpsimd.iota(my_place[:], pattern=[[P, SORTED_TILES]], base=0, channel_multiplier=1,
                           allow_small_or_imprecise_dtypes=True).then_inc(const_set, 1)
            nc.gpsimd.iota(tile_no[:], pattern=[[1, SORTED_TILES]], base=0, channel_multiplier=0,
                           allow_small_or_imprecise_dtypes=True).then_inc(const_set, 1)
            pool.wait_ge(attn_hi_set, 1)
            nc.gpsimd.tensor_tensor(wa_lo[:], attn_stage, f32(wa_hi[:]), ALU.subtract).then_inc(expert_lo_set, 1)
            with pool.Fori(0, GROUPS // 2) as k:
                for b in range(2):
                    pool.wait_ge(xn_set, 2 * k * GT + (b + 1) * GT)
                    nc.gpsimd.tensor_copy(rows[:, ds(2 * k * GT + b * GT, GT), 0:C],
                                          x_norm[:, b * GT:(b + 1) * GT, :]).then_inc(rows_kept, 1)
                    pool.wait_ge(experts_hi_set, 2)
                    nc.gpsimd.tensor_tensor(wx_lo[:, ds(2 * k + b, 1)], stage[:, ds(2 * k + b, 1)],
                                            f32(wx_hi[:, ds(2 * k + b, 1)]), ALU.subtract).then_inc(expert_lo_set, 1)

            pool.wait_ge(pads_out, 16)
            pool.wait_ge(places_set, 3)
            for g in range(GROUPS):
                for t in range(g * GT, (g + 1) * GT):
                    for place in (place1, place2):
                        nc.gpsimd.indirect_dma_start(
                            sorted_rows, bass.IndirectOffsetOnAxis(ap=place[:, t:t + 1], axis=0),
                            rows[:, t, :], None).then_inc(scattered[g], 16)
                if g >= 1:
                    pool.wait_ge(scattered[g - 1], 16 * TOPK * GT)
                    pool.sem_inc(rows_scattered, 1)
            pool.wait_ge(scattered[GROUPS - 1], 16 * TOPK * GT)
            pool.sem_inc(rows_scattered, 1)

            def scatter(i, r, first_half):
                pool.wait_ge(e_y_set[r % 2], first_half)
                pool.wait_ge(dest_set, i + 1)
                pool.sem_inc(scatter_ready, 1)
                nc.gpsimd.indirect_dma_start(
                    expert_rows, bass.IndirectOffsetOnAxis(ap=dest[:, r:r + 1], axis=0),
                    yring[:, r % YRING, :], None, bounds_check=last_row,
                    oob_is_err=False).then_inc(yring_out[r % YRING], 16)

            last_row = pool.to_reg(TOKENS * TOPK - 1)
            with pool.Fori(0, SORTED_TILES // XRING) as k:
                for r in range(XRING):
                    scatter(k * XRING + r, r, k * (XRING // 2) + r // 2 + 1)

        @block.scalar
        def _(act):
            act.dma_start(vec[:], vectors).then_inc(vec_in, 16)
            act.dma_start(bias_sb[:], bias).then_inc(vec_in, 16)
            act.dma_start(router_f[:], router).then_inc(router_in, 16)
            gu_stage = stage[:, :, 0:2 * KC * INNER].rearrange("p e (k u i) -> p e k u i", k=KC, u=2)
            for w, sem_, e in ((8, shared_in, 9), (0, experts_in, 8)):
                for k in range(KC):
                    act.dma_start(gu_stage[:, w:e, k, 0], w_gate[:, w:e, k, :]).then_inc(sem_, 16)
                    act.dma_start(gu_stage[:, w:e, k, 1], w_up[:, w:e, k, :]).then_inc(sem_, 16)
                act.dma_start(stage[:, w:e, 2 * KC * INNER:EW], w_down[:, w:e, :]).then_inc(sem_, 16)
                if w == 8:
                    act.dma_start(attn_stage, attn_w).then_inc(attn_in, 16)
            act.sem_inc(down_free, 1)
            for n in range(2):
                act.wait_ge(var_eps, n + 1)
                nc.scalar.activation(tmp_b[:], tmp_a[:], ACT.Sqrt).then_inc(root_set, 1)
            act.wait_ge(attn_in, 16)
            nc.scalar.copy(wa_hi[:], attn_stage).then_inc(attn_hi_set, 1)
            act.wait_ge(experts_in, 16 * (2 * KC + 1))
            for part in range(2):
                e = slice(4 * part, 4 * part + 4)
                nc.scalar.copy(wx_hi[:, e], stage[:, e]).then_inc(experts_hi_set, 1)

            def t_hi(g, b):
                act.wait_ge(t_done, g + 1)
                nc.scalar.copy(in_hi[:, b, :], bank[:, 0:2, :]).then_inc(thi_set, 1)

            def shared_group(g, b, first_, last_):
                act.wait_ge(gate_done, g + 1)
                if not first_:
                    act.wait_ge(h_set, g)
                nc.scalar.activation(silu_g, bank[:, 2, :], ACT.Silu).then_inc(silu_set, 1)
                if not last_:
                    if not first_:
                        act.wait_ge(logit_done, g)
                        act.wait_ge(up_done, g)
                    t_hi(g + 1, 1 - b)
                act.wait_ge(h_set, g + 1)
                nc.scalar.copy(mid_hi[:, b, :], h_shared).then_inc(hhi_set, 1)
                if not first_:
                    shared_store(g - 1)

            def shared_store(g):
                act.wait_ge(down_done, g + 1)
                act.wait_ge(expert_lo_set, 1)
                nc.scalar.copy(shared_out[:, ds(g * GT * C, GT * C)], bank[:, 5:7, :]).then_inc(down_free, 1)

            t_hi(0, 0)
            shared_group(0, 0, True, False)
            with act.Fori(0, (GROUPS - 2) // 2) as k:
                shared_group(2 * k + 1, 1, False, False)
                shared_group(2 * k + 2, 0, False, False)
            shared_group(GROUPS - 1, 1, False, True)
            shared_store(GROUPS - 1)

            act.wait_ge(logit_read, GROUPS)
            act.wait_ge(expert_lo_set, 1 + EXPERTS)
            nc.scalar.activation(route_tmp[1], logit, ACT.Sigmoid).then_inc(score_set, 1)
            act.wait_ge(vec_in, 32)
            nc.scalar.activation(decay[:], vec[:, v_decay, :], ACT.Sigmoid).then_inc(params_set, 1)
            nc.scalar.activation(first[:], vec[:, v_first, :], ACT.Exp).then_inc(params_set, 1)

            def set_z(g):
                for t in range(GT):
                    nc.scalar.mul(z[:, t, :], rows[:, g * GT + t, 0:C], rstd2[:, ds(g * GT + t, 1)]).then_inc(z_set, 1)

            def set_xt(g, b):
                act.wait_ge(zt_done, g + 1)
                for k in range(KC):
                    nc.scalar.activation(xt[b][:, k, 1:GROUP + 1], bank[:, k, :], ACT.Identity,
                                         bias=vec[:, ln_b, k:k + 1], scale=vec[:, ln_w, k:k + 1]).then_inc(xt_set, 1)

            def mix_hi(q, slot):
                act.wait_ge(mixed_set, 2 * q + 2)
                nc.scalar.copy(in_hi[:, slot, :], mixed).then_inc(mixhi_set, 1)

            def rwkv_hi(g):
                act.wait_ge(rwkv_set, g + 1)
                nc.scalar.copy(mid_hi[:], rwkv).then_inc(rwhi_set, 1)

            def mix_group(g, b, first_, last_):
                if not first_:
                    act.wait_ge(r_done, 2 * g)
                mix_hi(3 * g, (3 * b) % 2)
                if not last_:
                    if not first_:
                        act.wait_ge(mixed_set, 6 * g)
                    set_xt(g + 1, 1 - b)
                    if last_ is not None:
                        set_z(g + 2)
                if not first_:
                    rwkv_hi(g - 1)
                    act.wait_ge(v_done, g)
                mix_hi(3 * g + 1, (3 * b + 1) % 2)
                for k in range(KC):
                    act.wait_ge(r_done, 2 * g + k + 1)
                    nc.scalar.activation(r_gate[:, k * GROUP:(k + 1) * GROUP], bank[:, 6, :],
                                         ACT.Sigmoid).then_inc(r_set, 1)
                act.wait_ge(k_done, g + 1)
                mix_hi(3 * g + 2, (3 * b + 2) % 2)

            act.wait_ge(rstd2_set, 1)
            act.wait_ge(expert_lo_set, 1 + EXPERTS)
            act.wait_ge(hlo_set, GROUPS)
            set_z(0)
            set_xt(0, 0)
            set_z(1)
            act.wait_ge(logit_done, GROUPS)
            act.wait_ge(up_done, GROUPS)
            mix_group(0, 0, True, False)
            with act.Fori(0, (GROUPS - 4) // 2) as k:
                mix_group(2 * k + 1, 1, False, False)
                mix_group(2 * k + 2, 0, False, False)
            mix_group(GROUPS - 3, 1, False, False)
            mix_group(GROUPS - 2, 0, False, None)
            mix_group(GROUPS - 1, 1, False, True)
            rwkv_hi(GROUPS - 1)

            def step(s, u, half, peeled=False):
                def has(d):
                    return not peeled or 0 <= s - d < SORTED_TILES
                if has(0):
                    act.wait_ge(e_t_done, s + 1)
                    if has(2) :
                        act.wait_ge(e_gu_done, s - 1)
                    nc.scalar.copy(in_hi[:, u % 2, 0:C], bank[:, u % 2, 0:C]).then_inc(e_hi_set, 1)
                if has(1):
                    act.wait_ge(e_gu_done, s)
                    if has(3):
                        act.wait_ge(e_h_set, s - 2)
                    nc.scalar.activation(silu_t[:, (u - 1) % 2, :], bank[:, 2 + (u - 1) % 2, 0:INNER],
                                         ACT.Silu).then_inc(e_silu_set, 1)
                if has(2):
                    act.wait_ge(e_ht_done, s - 1)
                    if has(4):
                        act.wait_ge(e_down_done, s - 3)
                    nc.scalar.copy(mid_hi[:, u % 2, 0:INNER], bank[:, 4 + u % 2, 0:INNER]).then_inc(e_hhi_set, 1)
                if has(3) and (u - 3) % 2 == 0:
                    act.wait_ge(e_down_done, s - 2)
                    if has(3 + YRING):
                        act.wait_ge(yring_out[(u - 3) % YRING], 4 * (s - 3 - (u - 3) % YRING))
                    nc.scalar.copy(yring[:, (u - 3) % YRING, :], bank[:, 6, 0:C]).then_inc(e_y_set[0], 1)

            act.wait_ge(v_done, GROUPS)
            act.wait_ge(y_done, 2 * GROUPS)
            run_steps(act, step)

            def gate_group(g, b):
                act.wait_ge(y_in[b], 16 * g + 32 - 16 * b)
                for t in range(GT):
                    nc.scalar.mul(y_pair[:, b, t, 0:C], y_pair[:, b, t, 0:C],
                                  weight1[:, ds(g * GT + t, 1)]).then_inc(part_set, 1)
                act.wait_ge(sum_set, g + 1)
                nc.scalar.activation(acc, acc, ACT.Silu).then_inc(silu_y_set, 1)

            with act.Fori(0, GROUPS // 2) as k:
                for b in range(2):
                    gate_group(2 * k + b, b)

        def route(dve, link):
            def et(n):
                return route_tmp[n].rearrange("p (e t) -> p e t", e=EXPERTS)

            scores, choice, best = et(1), et(2), et(3)
            half = EXPERTS // 2
            dve.wait_ge(score_set, 1)
            dve.wait_ge(vec_in, 32)
            link(nc.vector.tensor_tensor(choice, scores, bias_sb[:].unsqueeze(2).to_broadcast([P, EXPERTS, TILES]), ALU.add))
            pairs = route_tmp[2].rearrange("p (h a t) -> p h a t", h=EXPERTS // 2, a=2)
            more = route_tmp[4].rearrange("p (h t) -> p h t", h=8)[:, 0:4]
            less = route_tmp[4].rearrange("p (h t) -> p h t", h=8)[:, 4:8]
            link(nc.vector.tensor_tensor(more, pairs[:, :, 0], pairs[:, :, 1], ALU.max))
            link(nc.vector.tensor_tensor(less, pairs[:, :, 0], pairs[:, :, 1], ALU.min))
            more2 = more.rearrange("p (n a) t -> p n a t", n=2)
            less2 = less.rearrange("p (n a) t -> p n a t", n=2)
            w = route_tmp[5].rearrange("p (x n t) -> p x n t", x=4, n=2)
            link(nc.vector.tensor_tensor(w[:, 0], more2[:, :, 0], more2[:, :, 1], ALU.max))
            link(nc.vector.tensor_tensor(w[:, 1], more2[:, :, 0], more2[:, :, 1], ALU.min))
            link(nc.vector.tensor_tensor(w[:, 2], less2[:, :, 0], less2[:, :, 1], ALU.max))
            link(nc.vector.tensor_tensor(w[:, 1], w[:, 1], w[:, 2], ALU.max))
            link(nc.vector.tensor_tensor(w[:, 0], w[:, 0], w[:, 1], ALU.add))
            link(nc.vector.tensor_tensor(w[:, 3, 1], w[:, 0, 1], w[:, 0, 0], ALU.is_gt))
            link(nc.vector.tensor_scalar(w[:, 3, 0], w[:, 3, 1], -1.0, 1.0, ALU.mult, ALU.add))
            for n in range(2):
                part = slice(n * half, (n + 1) * half)
                link(nc.vector.tensor_tensor(best[:, part], choice[:, part],
                                             w[:, 3, n].unsqueeze(1).to_broadcast([P, half, TILES]), ALU.mult))
            prefer = et(6)
            for e in range(EXPERTS):
                ins = nc.vector.memset(prefer[:, e, :], float(EXPERTS - e))
            link(ins)
            small = route_tmp[7].rearrange("p (x t) -> p x t", x=8)
            is_one, tmp = (et(8), et(9)), et(10)
            for n in range(TOPK):
                top = small[:, 0]
                link(nc.vector.tensor_reduce(top, best.rearrange("p e t -> p t e"), AX.X, ALU.max))
                link(nc.vector.tensor_tensor(tmp, best, top.unsqueeze(1).to_broadcast([P, EXPERTS, TILES]), ALU.is_equal))
                link(nc.vector.tensor_tensor(tmp, tmp, prefer, ALU.mult))
                link(nc.vector.tensor_reduce(top, tmp.rearrange("p e t -> p t e"), AX.X, ALU.max))
                link(nc.vector.tensor_tensor(is_one[n], tmp, top.unsqueeze(1).to_broadcast([P, EXPERTS, TILES]), ALU.is_equal))
                if n == 0:
                    link(nc.vector.scalar_tensor_tensor(best, is_one[0], REMOVED, best, ALU.mult, ALU.add))
            chosen = route_tmp[11].bitcast(BF16)[:, 0:ET]
            nc.vector.tensor_tensor(chosen, route_tmp[8], route_tmp[9], ALU.add).then_inc(chosen_set, 1)
            for n in range(TOPK):
                link(nc.vector.tensor_tensor(tmp, is_one[n], scores, ALU.mult))
                link(nc.vector.tensor_reduce(small[:, 1 + n], tmp.rearrange("p e t -> p t e"), AX.X, ALU.add))
            link(nc.vector.tensor_tensor(small[:, 3], small[:, 1], small[:, 2], ALU.add))
            link(nc.vector.tensor_scalar(small[:, 3], small[:, 3], 1e-20, None, ALU.add))
            link(nc.vector.reciprocal(small[:, 4], small[:, 3]))
            nc.vector.tensor_tensor(weight1[:], small[:, 1], small[:, 4], ALU.mult)
            nc.vector.tensor_tensor(weight2[:], small[:, 2], small[:, 4], ALU.mult)
            keep = et(12)
            nc.vector.memset(keep[:, :, 1:TILES], 1.0)
            link(nc.vector.memset(keep[:, :, 0:1], 0.0))
            dve.wait_ge(counted, 1)
            within, total = bank[:, 7, 0:ET], bank[:, 7, ET:2 * ET]
            link(nc.vector.tensor_tensor_scan(route_tmp[13], route_tmp[12], total, 0.0, ALU.mult, ALU.add))
            cnt = small[:, 5, 0:EXPERTS]
            tiles = small[:, 6, 0:EXPERTS]
            ends = small[:, 6, EXPERTS:2 * EXPERTS]
            starts = small[:, 6, 2 * EXPERTS:3 * EXPERTS]
            one8 = small[:, 5, EXPERTS:2 * EXPERTS]
            nc.vector.memset(one8, 1.0)
            link(nc.vector.tensor_scalar(int_tmp[:, 0:EXPERTS], et(13)[:, :, TILES - 1], float(P - 1), None, ALU.add))
            link(nc.vector.tensor_scalar(int_tmp[:, 0:EXPERTS], int_tmp[:, 0:EXPERTS], 7, None, ALU.logical_shift_right))
            link(nc.vector.tensor_copy(tiles, int_tmp[:, 0:EXPERTS]))
            link(nc.vector.tensor_tensor_scan(ends, one8, tiles, 0.0, ALU.mult, ALU.add))
            link(nc.vector.tensor_tensor(starts, ends, tiles, ALU.subtract))
            link(nc.vector.tensor_scalar(starts, starts, float(P), None, ALU.mult))
            place = et(13)
            link(nc.vector.tensor_tensor(route_tmp[13], route_tmp[13], total, ALU.subtract))
            link(nc.vector.tensor_tensor(route_tmp[13], within, route_tmp[13], ALU.add))
            link(nc.vector.tensor_tensor(place, place, starts.unsqueeze(2).to_broadcast([P, EXPERTS, TILES]), ALU.add))
            for n, to in enumerate((place1, place2)):
                link(nc.vector.tensor_tensor(tmp, is_one[n], place, ALU.mult))
                link(nc.vector.tensor_reduce(small[:, 1 + n], tmp.rearrange("p e t -> p t e"), AX.X, ALU.add))
                nc.vector.tensor_copy(to[:], small[:, 1 + n]).then_inc(places_set, 1)
            nc.vector.tensor_copy(rows[:, :, C + 1], small[:, 2])
            nc.vector.tensor_scalar(rows[:, :, C], my_place[:, 0:TILES], 2.0, None, ALU.mult).then_inc(places_set, 1)
            after = route_tmp[14].rearrange("p (e t) -> p e t", e=EXPERTS)
            for lo in (0, 32, 64):
                n = min(32, SORTED_TILES - lo)
                link(nc.vector.tensor_tensor(after[:, :, 0:n], tile_no[:, lo:lo + n].unsqueeze(1).to_broadcast([P, EXPERTS, n]),
                                             ends.unsqueeze(2).to_broadcast([P, EXPERTS, n]), ALU.is_ge))
                link(nc.vector.tensor_reduce(small[:, 7, 0:n], after[:, :, 0:n].rearrange("p e t -> p t e"), AX.X, ALU.add))
                link(nc.vector.tensor_scalar(weight_at[:, lo:lo + n], small[:, 7, 0:n], float(EXPERTS - 1), float(EW),
                                             ALU.min, ALU.mult))
            dve.sem_inc(places_set, 1)

        @block.vector
        def _(dve):
            steps = [0]

            def link(ins):
                steps[0] += 1
                ins.then_inc(dve_step, 1)
                dve.wait_ge(dve_step, steps[0])

            dve.wait_ge(router_in, 16)
            link(nc.vector.tensor_copy(wr_hi[:], router_f[:]))
            nc.vector.tensor_tensor(wr_lo[:], router_f[:], f32(wr_hi[:]), ALU.subtract).then_inc(shared_w_set, 1)

            for c in range(4):
                n = TILES // 4
                dve.wait_ge(x_in[c], 16)
                with dve.Fori(c * n, (c + 1) * n) as t:
                    nc.vector.bn_stats(stats[:, t, :], rows[:, t, 0:C]).then_inc(norm_set, 1)
            dve.wait_ge(norm_set, TILES)
            link(nc.vector.tensor_tensor(tmp_a[:], stats[:, :, 1], stats[:, :, 4], ALU.add))
            link(nc.vector.tensor_scalar(mean[:], tmp_a[:], 0.5, None, ALU.mult))
            link(nc.vector.tensor_tensor(tmp_a[:], stats[:, :, 1], stats[:, :, 4], ALU.subtract))
            link(nc.vector.tensor_tensor(tmp_a[:], tmp_a[:], tmp_a[:], ALU.mult))
            link(nc.vector.tensor_scalar(tmp_a[:], tmp_a[:], 0.25, None, ALU.mult))
            link(nc.vector.tensor_tensor(tmp_b[:], stats[:, :, 2], stats[:, :, 5], ALU.add))
            link(nc.vector.scalar_tensor_tensor(var[:], tmp_b[:], 1.0 / C, tmp_a[:], ALU.mult, ALU.add))

            def inverse_root(to, n):
                dve.wait_ge(root_set, n)
                link(nc.vector.reciprocal(to[:], tmp_b[:]))
                link(nc.vector.tensor_tensor(tmp_b[:], to[:], to[:], ALU.mult))
                link(nc.vector.tensor_tensor(tmp_b[:], tmp_b[:], tmp_a[:], ALU.mult))
                link(nc.vector.tensor_scalar(tmp_b[:], tmp_b[:], -0.5, 1.5, ALU.mult, ALU.add))
                link(nc.vector.tensor_tensor(to[:], to[:], tmp_b[:], ALU.mult))

            nc.vector.tensor_scalar(tmp_a[:], var[:], LN_EPS, None, ALU.add).then_inc(var_eps, 1)
            inverse_root(rstd, 1)
            link(nc.vector.tensor_tensor(tmp_a[:], var[:], rstd[:], ALU.mult))
            link(nc.vector.tensor_tensor(tmp_a[:], tmp_a[:], rstd[:], ALU.mult))
            link(nc.vector.tensor_scalar(tmp_a[:], tmp_a[:], LN_EPS, None, ALU.add))

            def set_xn(g, b, reused=True):
                if reused:
                    dve.wait_ge(t_done, g - 1)
                    dve.wait_ge(rows_kept, g - 1)
                for t in range(GT):
                    nc.vector.tensor_scalar(x_norm[:, b * GT + t, :], rows[:, g * GT + t, 0:C], mean[:, ds(g * GT + t, 1)], rstd[:, ds(g * GT + t, 1)],
                                            ALU.subtract, ALU.mult).then_inc(xn_set, 1)

            def t_lo(g, b):
                dve.wait_ge(thi_set, g + 1)
                nc.vector.tensor_tensor(in_lo[:, b, :], bank[:, 0:2, :].rearrange("p a c -> p (a c)"),
                                        f32(in_hi[:, b, :]), ALU.subtract).then_inc(tlo_set, 1)

            def shared_group(g, b, first_, last_, xn_ahead=True):
                dve.wait_ge(silu_set, g + 1)
                dve.wait_ge(up_done, g + 1)
                if not first_:
                    dve.wait_ge(hhi_set, g)
                    dve.wait_ge(hlo_set, g)
                nc.vector.tensor_tensor(h_shared, bank[:, 3, :], silu_g, ALU.mult).then_inc(h_set, 1)
                if not last_:
                    if not first_:
                        dve.wait_ge(logit_done, g)
                    t_lo(g + 1, 1 - b)
                dve.wait_ge(hhi_set, g + 1)
                nc.vector.tensor_tensor(mid_lo[:, b, :], h_shared, f32(mid_hi[:, b, :]),
                                        ALU.subtract).then_inc(hlo_set, 1)
                dve.wait_ge(logit_done, g + 1)
                nc.vector.tensor_copy(
                    logit.rearrange("p (e t) -> p e t", e=EXPERTS)[:, :, ds(g * GT, GT)],
                    bank[:, 4, 0:GT * EXPERTS].rearrange("p (t e) -> p e t", e=EXPERTS)).then_inc(logit_read, 1)
                if xn_ahead:
                    set_xn(g + 2, b)

            set_xn(0, 0, False)
            set_xn(1, 1, False)
            dve.sem_inc(var_eps, 1)
            inverse_root(rstd2, 2)
            dve.sem_inc(rstd2_set, 1)
            dve.wait_ge(shared_in, 16 * (2 * KC + 1))
            link(nc.vector.tensor_copy(wx_hi[:, SHARED], stage[:, SHARED]))
            nc.vector.tensor_tensor(wx_lo[:, SHARED], stage[:, SHARED], f32(wx_hi[:, SHARED]),
                                    ALU.subtract).then_inc(shared_w_set, 1)
            t_lo(0, 0)
            shared_group(0, 0, True, False)
            with dve.Fori(0, (GROUPS - 4) // 2) as k:
                shared_group(2 * k + 1, 1, False, False)
                shared_group(2 * k + 2, 0, False, False)
            shared_group(GROUPS - 3, 1, False, False)
            shared_group(GROUPS - 2, 0, False, False, xn_ahead=False)
            shared_group(GROUPS - 1, 1, False, True, xn_ahead=False)

            route(dve, link)

            dve.wait_ge(params_set, 2)
            link(nc.vector.memset(xt[0][:, :, 0:1], 0.0))

            def mixture(g, b, m, first_):
                q, slot = 3 * g + m, (3 * b + m) % 2
                which = (mk, mr, mv)[m]
                if not (first_ and m == 0):
                    dve.wait_ge(mixhi_set, q)
                    dve.wait_ge(mixlo_set, q)
                for k in range(KC):
                    cols = slice(k * GROUP, (k + 1) * GROUP)
                    nc.vector.scalar_tensor_tensor(mixed[:, cols], diff[:, cols], vec[:, which, k:k + 1],
                                                   xt[b][:, k, 0:GROUP], ALU.mult, ALU.add).then_inc(mixed_set, 1)
                dve.wait_ge(mixhi_set, q + 1)
                nc.vector.tensor_tensor(in_lo[:, slot, :], mixed, f32(in_hi[:, slot, :]),
                                        ALU.subtract).then_inc(mixlo_set, 1)

            def differences(g, b, odd_count):
                dve.wait_ge(xt_set, 2 * g + 2)
                if b == 1:
                    nc.vector.tensor_copy(xt[1][:, :, 0:1], xt[0][:, :, GROUP:GROUP + 1]).then_inc(edge_set, 1)
                    dve.wait_ge(edge_set, odd_count)
                nc.vector.tensor_tensor(diff.rearrange("p (k t) -> p k t", k=KC), xt[b][:, :, 1:GROUP + 1],
                                        xt[b][:, :, 0:GROUP], ALU.subtract).then_inc(diff_set, 1)
                dve.wait_ge(diff_set, g + 1)

            def after_projection(g, b):
                dve.wait_ge(k_done, g + 1)
                for k in range(KC):
                    cols = slice(k * GROUP, (k + 1) * GROUP)
                    nc.vector.tensor_tensor_scan(s_state[:, cols], decay[:, k:k + 1].to_broadcast([P, GROUP]),
                                                 bank[:, 2 + k, :], 0.0 if b == 0 else last_s[:, k:k + 1],
                                                 ALU.mult, ALU.add).then_inc(scan_set, 1)
                for k in range(KC):
                    cols = slice(k * GROUP, (k + 1) * GROUP)
                    dve.wait_ge(scan_set, 2 * g + k + 1)
                    nc.vector.scalar_tensor_tensor(rwkv[:, cols], s_state[:, cols], first[:, k:k + 1],
                                                   bank[:, 2 + k, :], ALU.mult, ALU.add).then_inc(k_read, 1)
                nc.vector.tensor_copy(last_s[:], s_state.rearrange("p (k t) -> p k t", k=KC)[:, :, GROUP - 1])
                dve.wait_ge(k_read, 2 * g + 2)
                dve.wait_ge(v_done, g + 1)
                nc.vector.tensor_tensor(rwkv, rwkv, bank[:, 4:6, :].rearrange("p a c -> p (a c)"),
                                        ALU.mult).then_inc(v_read, 1)
                dve.wait_ge(v_read, g + 1)
                dve.wait_ge(r_set, 2 * g + 2)
                nc.vector.tensor_tensor(rwkv, rwkv, r_gate, ALU.mult).then_inc(rwkv_set, 1)
                dve.wait_ge(rwhi_set, g + 1)
                nc.vector.tensor_tensor(mid_lo[:].rearrange("p a c -> p (a c)"), rwkv,
                                        f32(mid_hi[:].rearrange("p a c -> p (a c)")),
                                        ALU.subtract).then_inc(rwlo_set, 1)

            def add_y(g):
                dve.wait_ge(rows_scattered, g + 1)
                for pair in range(2):
                    dve.wait_ge(y_done, 2 * g + pair + 1)
                    row = rows[:, ds(g * GT + 2 * pair, 2), 0:C]
                    nc.vector.tensor_tensor(row, bank[:, 7 if pair == 0 else 0, :].rearrange(
                        "p (t c) -> p t c", t=2), row, ALU.add).then_inc(s_set, 1)

            def mix_group(g, b, first_, odd_count=None):
                differences(g, b, odd_count)
                mixture(g, b, 0, first_)
                if not first_:
                    after_projection(g - 1, 1 - b)
                mixture(g, b, 1, first_)
                if not first_:
                    add_y(g - 1)
                mixture(g, b, 2, first_)

            mix_group(0, 0, True)
            with dve.Fori(0, (GROUPS - 2) // 2) as k:
                mix_group(2 * k + 1, 1, False, k + 1)
                mix_group(2 * k + 2, 0, False)
            mix_group(GROUPS - 1, 1, False, GROUPS // 2)
            after_projection(GROUPS - 1, 1)
            add_y(GROUPS - 1)

            def step(s, u, half, peeled=False):
                def has(d):
                    return not peeled or 0 <= s - d < SORTED_TILES
                if has(0):
                    dve.wait_ge(e_hi_set, s + 1)
                    nc.vector.tensor_tensor(in_lo[:, u % 2, 0:C], bank[:, u % 2, 0:C], f32(in_hi[:, u % 2, 0:C]),
                                            ALU.subtract).then_inc(e_lo_set, 1)
                    slot = u % XRING
                    dve.wait_ge(xring_in[slot], 2 * s + 16 - 2 * slot)
                    if has(XRING):
                        dve.wait_ge(yring_out[slot % YRING], 4 * (s - XRING - slot % YRING) + 16)
                    nc.vector.scalar_tensor_tensor(dest[:, slot:slot + 1], xring[:, slot, C + 1:C + 2],
                                                   my_place[:, ds(s, 1)], xring[:, slot, C:C + 1],
                                                   ALU.is_equal, ALU.add).then_inc(dest_set, 1)
                if has(1):
                    dve.wait_ge(e_silu_set, s)
                    if has(3):
                        dve.wait_ge(e_ht_done, s - 2)
                    nc.vector.tensor_tensor(h_t[:, (u - 1) % 2, :], bank[:, 2 + (u - 1) % 2, INNER:2 * INNER],
                                            silu_t[:, (u - 1) % 2, :], ALU.mult).then_inc(e_h_set, 1)
                if has(2):
                    dve.wait_ge(e_hhi_set, s - 1)
                    nc.vector.tensor_tensor(mid_lo[:, u % 2, 0:INNER], bank[:, 4 + u % 2, 0:INNER],
                                            f32(mid_hi[:, u % 2, 0:INNER]), ALU.subtract).then_inc(e_hlo_set, 1)
                if has(3) and (u - 3) % 2 == 1:
                    dve.wait_ge(e_down_done, s - 2)
                    if has(3 + YRING):
                        dve.wait_ge(yring_out[(u - 3) % YRING], 4 * (s - 3 - (u - 3) % YRING))
                    nc.vector.tensor_copy(yring[:, (u - 3) % YRING, :], bank[:, 7, 0:C]).then_inc(e_y_set[1], 1)

            run_steps(dve, step)

            def gate_group(g, b):
                for t in range(GT):
                    dve.wait_ge(part_set, g * GT + t + 1)
                    nc.vector.scalar_tensor_tensor(acc[:, t, :], y_pair[:, b, t, C:2 * C],
                                                   weight2[:, ds(g * GT + t, 1)], y_pair[:, b, t, 0:C],
                                                   ALU.mult, ALU.add).then_inc(routed_set, 1)
                dve.wait_ge(routed_set, g * GT + GT)
                flat = acc.rearrange("p t c -> p (t c)")
                nc.vector.tensor_tensor(flat, flat, shared_out[:, ds(g * GT * C, GT * C)], ALU.add).then_inc(sum_set, 1)
                dve.wait_ge(silu_y_set, g + 1)
                nc.vector.tensor_tensor(acc, acc, rows[:, ds(g * GT, GT), 0:C], ALU.mult).then_inc(gated_set, 1)
                dve.wait_ge(gated_set, g + 1)
                nc.vector.tensor_tensor(x_again[:, b], x_again[:, b], acc, ALU.add).then_inc(out_set, 1)
                dve.wait_ge(out_set, g + 1)

            with dve.Fori(0, GROUPS // 2) as k:
                for b in range(2):
                    gate_group(2 * k + b, b)

        @block.tensor
        def _(pe):
            pe.wait_ge(const_set, 6)

            def product(out_ap, hi_l, lo_l, hi_r, lo_r, first_, last_, lolo=False):
                nc.tensor.matmul(out_ap, hi_l, hi_r, start=first_, stop=False)
                nc.tensor.matmul(out_ap, hi_l, lo_r, start=False, stop=False)
                if lolo:
                    nc.tensor.matmul(out_ap, lo_l, lo_r, start=False, stop=False)
                return nc.tensor.matmul(out_ap, lo_l, hi_r, start=False, stop=last_)

            def transposes(g, b):
                pe.wait_ge(xn_set, GT * (g + 1))
                for k in range(KC):
                    for t in range(GT):
                        mm = nc.tensor.transpose(bank[:, k, t * P:(t + 1) * P],
                                                 x_norm[:, b * GT + t, k * P:(k + 1) * P], ident[:])
                mm.then_inc(t_done, 1)

            def gate_up(g, b):
                pe.wait_ge(thi_set, g + 1)
                pe.wait_ge(tlo_set, g + 1)
                for n, done in ((0, gate_done), (1, up_done)):
                    for k in range(KC):
                        cols = slice((2 * k + n) * INNER, (2 * k + n + 1) * INNER)
                        tok = slice(k * GROUP, (k + 1) * GROUP)
                        mm = product(bank[:, 2 + n, :], wx_hi[:, SHARED, cols], wx_lo[:, SHARED, cols],
                                     in_hi[:, b, tok], in_lo[:, b, tok], k == 0, k == KC - 1)
                    mm.then_inc(done, 1)

            def down(g, b):
                pe.wait_ge(hhi_set, g + 1)
                pe.wait_ge(hlo_set, g + 1)
                pe.wait_ge(down_free, g + 1)
                for t in range(GT):
                    tok = slice(t * P, (t + 1) * P)
                    mm = product(bank[:, 5 + t // 2, (t % 2) * C:(t % 2 + 1) * C],
                                 mid_hi[:, b, tok], mid_lo[:, b, tok],
                                 wx_hi[:, SHARED, EW - C:EW], wx_lo[:, SHARED, EW - C:EW], True, True)
                mm.then_inc(down_done, 1)

            def logits(g, b, first_):
                if not first_:
                    pe.wait_ge(logit_read, g)
                for t in range(GT):
                    for k in range(KC):
                        tok = slice(k * GROUP + t * P, k * GROUP + (t + 1) * P)
                        mm = product(bank[:, 4, t * EXPERTS:(t + 1) * EXPERTS], in_hi[:, b, tok], in_lo[:, b, tok],
                                     wr_hi[:, k, :], wr_lo[:, k, :], k == 0, k == KC - 1, lolo=True)
                mm.then_inc(logit_done, 1)

            def shared_group(g, b, first_, last_):
                if not last_:
                    pe.wait_ge(thi_set, g + 1)
                    pe.wait_ge(tlo_set, g + 1)
                    transposes(g + 1, 1 - b)
                if not first_:
                    down(g - 1, 1 - b)
                logits(g, b, first_)
                if not last_:
                    pe.wait_ge(silu_set, g + 1)
                    pe.wait_ge(h_set, g + 1)
                    gate_up(g + 1, 1 - b)

            transposes(0, 0)
            pe.wait_ge(shared_w_set, 2)
            gate_up(0, 0)
            shared_group(0, 0, True, False)
            with pe.Fori(0, (GROUPS - 2) // 2) as k:
                shared_group(2 * k + 1, 1, False, False)
                shared_group(2 * k + 2, 0, False, False)
            shared_group(GROUPS - 1, 1, False, True)
            down(GROUPS - 1, 1)

            pe.wait_ge(chosen_set, 1)
            chosen = route_tmp[11].bitcast(BF16)[:, 0:ET]
            nc.tensor.matmul(bank[:, 7, 0:ET], before[:], chosen, start=True, stop=True)
            nc.tensor.matmul(bank[:, 7, ET:2 * ET], ones[:], chosen, start=True, stop=True).then_inc(counted, 1)

            def z_transposes(g):
                pe.wait_ge(z_set, GT * (g + 1))
                for k in range(KC):
                    for t in range(GT):
                        mm = nc.tensor.transpose(bank[:, k, t * P:(t + 1) * P], z[:, t, k * P:(k + 1) * P], ident[:])
                mm.then_inc(zt_done, 1)

            def project(w, d, bank_no, slot):
                for k in range(KC):
                    cols = slice(d * P, (d + 1) * P)
                    tok = slice(k * GROUP, (k + 1) * GROUP)
                    mm = product(bank[:, bank_no, :], wa_hi[:, w, k, cols], wa_lo[:, w, k, cols],
                                 in_hi[:, slot, tok], in_lo[:, slot, tok], k == 0, k == KC - 1)
                return mm

            def mixture_ready(q):
                pe.wait_ge(mixhi_set, q + 1)
                pe.wait_ge(mixlo_set, q + 1)

            def y_out(g):
                pe.wait_ge(rwhi_set, g + 1)
                pe.wait_ge(rwlo_set, g + 1)
                for pair in range(2):
                    for t in range(2):
                        for k in range(KC):
                            tok = slice((2 * pair + t) * P, (2 * pair + t + 1) * P)
                            mm = product(bank[:, 7 if pair == 0 else 0, t * C:(t + 1) * C],
                                         mid_hi[:, k, tok], mid_lo[:, k, tok],
                                         wa_hi[:, 3, k, :], wa_lo[:, 3, k, :], k == 0, k == KC - 1)
                    mm.then_inc(y_done, 1)

            def mix_group(g, b, first_, last_):
                if not last_:
                    pe.wait_ge(xt_set, 2 * g + 2)
                    z_transposes(g + 1)
                mixture_ready(3 * g)
                if not first_:
                    pe.wait_ge(k_read, 2 * g)
                for d in range(KC):
                    mm = project(0, d, 2 + d, (3 * b) % 2)
                mm.then_inc(k_done, 1)
                if not first_:
                    if not last_:
                        pe.wait_ge(xt_set, 2 * g + 4)
                    y_out(g - 1)
                mixture_ready(3 * g + 1)
                for d in range(KC):
                    if not (first_ and d == 0):
                        pe.wait_ge(r_set, 2 * g + d)
                    mm = project(2, d, 6, (3 * b + 1) % 2)
                    mm.then_inc(r_done, 1)
                mixture_ready(3 * g + 2)
                if not first_:
                    pe.wait_ge(v_read, g)
                for d in range(KC):
                    mm = project(1, d, 4 + d, (3 * b + 2) % 2)
                mm.then_inc(v_done, 1)

            z_transposes(0)
            pe.wait_ge(expert_lo_set, 1)
            pe.wait_ge(logit_read, GROUPS)
            pe.wait_ge(down_free, GROUPS + 1)
            mix_group(0, 0, True, False)
            with pe.Fori(0, (GROUPS - 2) // 2) as k:
                mix_group(2 * k + 1, 1, False, False)
                mix_group(2 * k + 2, 0, False, False)
            mix_group(GROUPS - 1, 1, False, True)
            y_out(GROUPS - 1)
            pe.wait_ge(s_set, 2 * GROUPS)

            pe.wait_ge(places_set, 4)
            pe.wait_ge(expert_lo_set, 1 + EXPERTS)

            wx_hi_flat = wx_hi[:].rearrange("p e w -> p (e w)")
            wx_lo_flat = wx_lo[:].rearrange("p e w -> p (e w)")

            def weights_at(s):
                return pe.value_load(weight_at[0:1, ds(s, 1)], min_val=0, max_val=(EXPERTS - 1) * EW)

            def step(s, u, half, peeled=False):
                def has(d):
                    return not peeled or 0 <= s - d < SORTED_TILES
                if has(0):
                    slot = u % XRING
                    pe.wait_ge(xring_in[slot], 2 * s + 16 - 2 * slot)
                    if has(2):
                        pe.wait_ge(e_lo_set, s - 1)
                    for k in range(KC):
                        mm = nc.tensor.transpose(bank[:, u % 2, k * P:(k + 1) * P],
                                                 xring[:, slot, k * P:(k + 1) * P], ident[:])
                    mm.then_inc(e_t_done, 1)
                if has(1):
                    v = weights_at(s - 1)
                    pe.wait_ge(e_lo_set, s)
                    if has(3):
                        pe.wait_ge(e_h_set, s - 2)
                    b = (u - 1) % 2
                    for k in range(KC):
                        tok = slice(k * P, (k + 1) * P)
                        mm = product(bank[:, 2 + b, 0:2 * INNER], in_hi[:, b, tok], in_lo[:, b, tok],
                                     wx_hi_flat[:, ds(v + k * 2 * INNER, 2 * INNER)],
                                     wx_lo_flat[:, ds(v + k * 2 * INNER, 2 * INNER)], k == 0, k == KC - 1)
                    mm.then_inc(e_gu_done, 1)
                if has(2):
                    pe.wait_ge(e_h_set, s - 1)
                    if has(4):
                        pe.wait_ge(e_hlo_set, s - 3)
                    nc.tensor.transpose(bank[:, 4 + u % 2, 0:P], h_t[:, u % 2, :], ident[:]).then_inc(e_ht_done, 1)
                if has(3):
                    v = weights_at(s - 3)
                    pe.wait_ge(e_hlo_set, s - 2)
                    b = (u - 3) % 2
                    if has(5):
                        pe.wait_ge(e_y_set[b], half)
                    product(bank[:, 6 + b, 0:C], mid_hi[:, b, 0:INNER], mid_lo[:, b, 0:INNER],
                            wx_hi_flat[:, ds(v + 2 * KC * INNER, C)],
                            wx_lo_flat[:, ds(v + 2 * KC * INNER, C)], True, True).then_inc(e_down_done, 1)

            run_steps(pe, step)


def kernel(**inputs):
    import numpy as np
    import concourse.bacc as bacc
    from concourse.bass_utils import run_bass_kernel_spmd

    given = {name.removeprefix("L0_"): np.asarray(a) for name, a in inputs.items()}

    def chunks(a):
        return a.reshape(KC, P, -1).transpose(1, 0, 2)

    vectors = np.stack([given["attn_" + n].reshape(KC, P).T for n in
                        ("time_mix_k", "time_mix_v", "time_mix_r", "time_decay", "time_first", "ln_w", "ln_b")], 1)
    experts = [np.concatenate([given["ffn_w_" + n], given["ffn_sw_" + n][None]]) for n in ("gate", "up", "down")]
    arrays = {
        "x": given["attn_x"],
        "vectors": vectors,
        "bias": np.broadcast_to(given["ffn_correction_bias"], (P, EXPERTS)),
        "router": chunks(given["ffn_router_weight"].T),
        "attn_w": np.stack([chunks(given["attn_" + n].T) for n in ("Wk", "Wv", "Wr", "Wo")], 1),
        "w_gate": experts[0].reshape(EXPERTS + 1, KC, P, INNER).transpose(2, 0, 1, 3),
        "w_up": experts[1].reshape(EXPERTS + 1, KC, P, INNER).transpose(2, 0, 1, 3),
        "w_down": experts[2].transpose(1, 0, 2),
    }
    arrays = {name: np.ascontiguousarray(a) for name, a in arrays.items()}
    nc = bacc.Bacc("TRN2", target_bir_lowering=False, num_devices=1)
    args = [nc.dram_tensor(name, a.shape, F32, kind="ExternalInput").ap() for name, a in arrays.items()]
    out = nc.dram_tensor("out", (BATCH, SEQ, C), F32, kind="ExternalOutput").ap()
    gated_time_mix_kernel(nc, *args, out)
    result = run_bass_kernel_spmd(nc, [arrays], core_ids=[0])
    return result.results[0]["out"]
```

```python
from contextlib import ExitStack

import concourse.bass as bass
from concourse import mybir

F32 = mybir.dt.float32
F32R = mybir.dt.float32r
BF16 = mybir.dt.bfloat16
I32 = mybir.dt.int32
U32 = mybir.dt.uint32
ALU = mybir.AluOpType
ACT = mybir.ActivationFunctionType
AX = mybir.AxisListType
ds = bass.ds

P = 128
BATCH, SEQ, C = 4, 1024, 256
TOKENS = BATCH * SEQ
KC = C // P
EXPERTS, INNER, TOPK = 8, 128, 2
TILES = TOKENS // P
GROUP = 512
GT = GROUP // P
GROUPS = TOKENS // GROUP
ROW = C + 2
SORTED_TILES = TOKENS * TOPK // P + EXPERTS
SORTED_ROWS = SORTED_TILES * P
EW = 2 * KC * INNER + C
SHARED = EXPERTS
LN_EPS = 1e-5
OUT_OF_RANGE = float(TOKENS * TOPK)
REMOVED = -1e30
XRING, YRING = 8, 8


def half_tiles(s):
    return (s - 5) // 2 + 1

def run_steps(eng, step, load_weights=None):
    load_weights and load_weights(0, 0, XRING - 1)
    for s in range(XRING):
        step(s, s, half_tiles(s), True)
    with eng.Fori(0, SORTED_TILES // XRING - 1) as k:
        load_weights and load_weights(k * XRING + XRING - 3, XRING - 3, XRING + 2)
        for u in range(XRING):
            step(k * XRING + XRING + u, u + XRING, k * (XRING // 2) + half_tiles(u + XRING))
    load_weights and load_weights(SORTED_TILES - 3, SORTED_TILES - 3, 3)
    for s in range(SORTED_TILES, SORTED_TILES + 3):
        step(s, s, half_tiles(s), True)


def gated_time_mix_kernel(nc, x, vectors, bias, router, wk_wo, wr_wv, expert_w, out):
    sorted_rows = nc.dram_tensor("sorted_rows", [SORTED_ROWS, ROW], F32).ap()
    expert_rows = nc.dram_tensor("expert_rows", [TOKENS * TOPK, C], F32).ap()
    x_tiles = x.rearrange("b (j p) c -> p (b j) c", p=P)
    out_tiles = out.rearrange("b (j p) c -> p (b j) c", p=P)
    expert_tiles = expert_rows.rearrange("(j p k) c -> p j (k c)", p=P, k=TOPK)

    with ExitStack() as ctx:
        def sb(name, shape, dt=F32):
            return ctx.enter_context(nc.sbuf_tensor(name, shape, dt))

        def sem(name):
            return ctx.enter_context(nc.semaphore(name))

        rows = sb("rows", [P, TILES, ROW])
        shared_out = sb("shared_out", [P, TILES * C])
        wx_hi = sb("wx_hi", [P, EXPERTS + 1, EW], F32R)
        wx_lo = sb("wx_lo", [P, EXPERTS + 1, EW], F32R)
        wa_hi = sb("wa_hi", [P, 2, KC, C], F32R)
        wa_lo = sb("wa_lo", [P, 2, KC, C], F32R)
        wa = sb("wa", [P, 2, KC, C])
        wr_hi = sb("wr_hi", [P, KC, EXPERTS], F32R)
        wr_lo = sb("wr_lo", [P, KC, EXPERTS], F32R)
        in_hi = sb("in_hi", [P, 2, KC * GROUP], F32R)
        in_lo = sb("in_lo", [P, 2, KC * GROUP], F32R)
        mid_hi = sb("mid_hi", [P, 2, GROUP], F32R)
        mid_lo = sb("mid_lo", [P, 2, GROUP], F32R)

        xring = sb("xring", [P, XRING, ROW])
        pad_row = sb("pad_row", [P, ROW])
        dest = sb("dest", [P, XRING], U32)
        vec = sb("vec", [P, 7, KC])
        mk, mv, mr, v_decay, v_first, ln_w, ln_b = range(7)
        bias_sb = sb("bias_sb", [P, EXPERTS])
        router_f = sb("router_f", [P, KC, EXPERTS])
        decay = sb("decay", [P, KC])
        first = sb("first", [P, KC])
        stats = sb("stats", [P, TILES, 6])
        mean = sb("mean", [P, TILES])
        var = sb("var", [P, TILES])
        rstd = sb("rstd", [P, TILES])
        rstd2 = sb("rstd2", [P, TILES])
        tmp_a = sb("tmp_a", [P, TILES])
        tmp_b = sb("tmp_b", [P, TILES])
        ident = sb("ident", [P, P])
        before = sb("before", [P, P], BF16)
        ones = sb("ones", [P, P], BF16)
        place1 = sb("place1", [P, TILES], U32)
        place2 = sb("place2", [P, TILES], U32)
        weight1 = sb("weight1", [P, TILES])
        weight2 = sb("weight2", [P, TILES])
        my_place = sb("my_place", [P, SORTED_TILES])
        tile_no = sb("tile_no", [P, SORTED_TILES])
        weight_at = sb("weight_at", [P, SORTED_TILES], I32)
        int_tmp = sb("int_tmp", [P, SORTED_TILES], I32)
        last_s = sb("last_s", [P, KC])

        scratch = sb("scratch", [P, 8196])
        shared_end = TILES * C
        attn_stage = shared_out[:, shared_end - 2 * KC * C:shared_end].rearrange(
            "p (w k c) -> p w k c", w=2, k=KC)
        stage = scratch[:, 0:9 * EW].rearrange("p (e w) -> p e w", e=9)
        silu_g = scratch[:, 9 * EW:9 * EW + GROUP]
        h_shared = scratch[:, 9 * EW + GROUP:9 * EW + 2 * GROUP]
        GK = KC * GROUP
        z = scratch[:, 0:GK].rearrange("p (t c) -> p t c", t=GT)
        xt = [scratch[:, GK + h * KC * (GROUP + 1):GK + (h + 1) * KC * (GROUP + 1)].rearrange(
            "p (k t) -> p k t", k=KC) for h in range(2)]
        at = GK + 2 * KC * (GROUP + 1)
        diff = [scratch[:, at:at + GK], sb("diff_odd", [P, GK])[:]]
        mix_k = scratch[:, at + GK:at + 2 * GK]
        rwkv = scratch[:, at + 2 * GK:at + 3 * GK]
        y_new = scratch[:, at + 3 * GK:at + 4 * GK]
        r_gate = scratch[:, at + 4 * GK:at + 5 * GK]
        xring_flat = xring[:].rearrange("p r c -> p (r c)")
        mix_r, mix_v = xring_flat[:, 0:GK], xring_flat[:, GK:2 * GK]
        ET = EXPERTS * TILES
        route_tmp = [scratch[:, at + GK + n * ET:at + GK + (n + 1) * ET] for n in range(15)]
        logit = scratch[:, 9 * EW + 2 * GROUP:9 * EW + 2 * GROUP + ET]
        silu_t = scratch[:, 7172:7172 + 2 * INNER].rearrange("p (b i) -> p b i", b=2)
        h_t = scratch[:, 7172 + 2 * INNER:7172 + 4 * INNER].rearrange("p (b i) -> p b i", b=2)
        yring = scratch[:, 0:YRING * C].rearrange("p (r c) -> p r c", r=YRING)
        y_pair = scratch[:, 0:4 * GK].rearrange("p (b t c) -> p b t c", b=2, t=GT)
        x_again = scratch[:, 4 * GK:6 * GK].rearrange("p (b t c) -> p b t c", b=2, t=GT)
        acc = scratch[:, 6 * GK:7 * GK].rearrange("p (t c) -> p t c", t=GT)
        x_norm = xring[:, :, 0:C]

        bank = ctx.enter_context(nc.psum_tensor("bank", [P, 8, GROUP], F32))

        x_in = [sem(f"x_in{c}") for c in range(4)]
        rows_kept = sem("rows_kept")
        vec_in, router_in, shared_in = sem("vec_in"), sem("router_in"), sem("shared_in")
        attn_in, experts_in, wa_in = sem("attn_in"), sem("experts_in"), sem("wa_in")
        pads_out = sem("pads_out")
        scattered = [sem(f"scattered{g}") for g in range(GROUPS)]
        xring_in = [sem(f"xring_in{r}") for r in range(XRING)]
        yring_out = [sem(f"yring_out{r}") for r in range(YRING)]
        y_in = [sem(f"y_in{b}") for b in range(2)]
        out_out = [sem(f"out_out{b}") for b in range(2)]
        pad_set, const_set, edge_zero = sem("pad_set"), sem("const_set"), sem("edge_zero")
        attn_hi_set, attn_lo_set = sem("attn_hi_set"), sem("attn_lo_set")
        experts_hi_set, experts_lo_set = sem("experts_hi_set"), sem("experts_lo_set")
        shared_w_set, params_set = sem("shared_w_set"), sem("params_set")
        dve_step = sem("dve_step")
        var_eps, root_set, norm_set = sem("var_eps"), sem("root_set"), sem("norm_set")
        rstd2_set = sem("rstd2_set")
        xn_set, t_done, thi_set, tlo_set = sem("xn_set"), sem("t_done"), sem("thi_set"), sem("tlo_set")
        gate_done, up_done, silu_set, h_set = sem("gate_done"), sem("up_done"), sem("silu_set"), sem("h_set")
        hhi_set, hlo_set, down_done, down_free = sem("hhi_set"), sem("hlo_set"), sem("down_done"), sem("down_free")
        logit_done, logit_read = sem("logit_done"), sem("logit_read")
        score_set, chosen_set, counted, places_set = sem("score_set"), sem("chosen_set"), sem("counted"), sem("places_set")
        z_set, zt_done, xt_set = sem("z_set"), sem("zt_done"), sem("xt_set")
        edge_set, diff_set = sem("edge_set"), sem("diff_set")
        mix_k_set, mix_r_set, mix_v_set = sem("mix_k_set"), sem("mix_r_set"), sem("mix_v_set")
        k_hi_set, k_lo_set, k_done = sem("k_hi_set"), sem("k_lo_set"), sem("k_done")
        r_done, r_set, v_done = sem("r_done"), sem("r_set"), sem("v_done")
        scan_set, k_read, v_read, rwkv_set = sem("scan_set"), sem("k_read"), sem("v_read"), sem("rwkv_set")
        rwhi_set, rwlo_set, y_done = sem("rwhi_set"), sem("rwlo_set"), sem("y_done")
        last_set = sem("last_set")
        y_copied, s_set = sem("y_copied"), sem("s_set")
        e_t_done, e_hi_set, e_lo_set, e_gu_done = sem("e_t_done"), sem("e_hi_set"), sem("e_lo_set"), sem("e_gu_done")
        e_silu_set, e_h_set, e_ht_done = sem("e_silu_set"), sem("e_h_set"), sem("e_ht_done")
        e_hhi_set, e_hlo_set, e_down_done = sem("e_hhi_set"), sem("e_hlo_set"), sem("e_down_done")
        e_y_set = [sem("e_y_even_set"), sem("e_y_odd_set")]
        dest_set, scatter_ready = sem("dest_set"), sem("scatter_ready")
        part_set, routed_set, sum_set, silu_y_set = sem("part_set"), sem("routed_set"), sem("sum_set"), sem("silu_y_set")
        gated_set, out_set = sem("gated_set"), sem("out_set")

        block = ctx.enter_context(nc.Block())

        def f32(ap):
            return ap.bitcast(F32)

        @block.sync
        def _(sp):
            for c in range(4):
                n = TILES // 4
                sp.dma_start(rows[:, c * n:(c + 1) * n, 0:C], x_tiles[:, c * n:(c + 1) * n, :]).then_inc(x_in[c], 16)
                if c == 0:
                    sp.dma_start(stage[:, SHARED], expert_w[:, SHARED]).then_inc(shared_in, 16)
            sp.dma_start(attn_stage, wk_wo).then_inc(attn_in, 16)
            for e in range(0, EXPERTS, 4):
                sp.dma_start(stage[:, e:e + 4], expert_w[:, e:e + 4]).then_inc(experts_in, 16)
            sp.dma_start(wa[:], wr_wv).then_inc(wa_in, 16)
            sp.wait_ge(pad_set, 3)
            sp.wait_ge(wa_in, 16)
            sp.dma_start(sorted_rows.rearrange("(i p) c -> p i c", p=P),
                         pad_row[:].unsqueeze(1).to_broadcast([P, SORTED_TILES, ROW])).then_inc(pads_out, 16)

            for g in range(GROUPS):
                sp.wait_ge(scattered[g], 16 * TOPK * GT)
            sp.wait_ge(r_done, 2 * GROUPS)
            sp.wait_ge(v_done, 2 * GROUPS)

            def load_sorted(i, slot, reused):
                if reused:
                    sp.wait_ge(e_t_done, i - XRING + 1)
                    sp.wait_ge(dest_set, i - XRING + 1)
                sp.dma_start(xring[:, slot, :], sorted_rows[ds(i * P, P), :]).then_inc(xring_in[slot], 16)

            for r in range(XRING):
                load_sorted(r, r, False)
            with sp.Fori(0, SORTED_TILES // XRING - 1) as k:
                for r in range(XRING):
                    load_sorted(k * XRING + XRING + r, r, True)

            for n in range(YRING):
                sp.wait_ge(yring_out[n], 16 * (SORTED_TILES // YRING))

            def load_group(g, b, reused):
                if reused:
                    sp.wait_ge(out_set, g - 1)
                sp.dma_start(y_pair[:, b], expert_tiles[:, ds(g * GT, GT), :]).then_inc(y_in[b], 16)
                if reused:
                    sp.wait_ge(out_out[b], 8 * (g - b))
                sp.dma_start(x_again[:, b], x_tiles[:, ds(g * GT, GT), :]).then_inc(y_in[b], 16)

            def store_group(g, b):
                sp.wait_ge(out_set, g + 1)
                sp.dma_start(out_tiles[:, ds(g * GT, GT), :], x_again[:, b]).then_inc(out_out[b], 16)

            load_group(0, 0, False)
            load_group(1, 1, False)
            with sp.Fori(0, GROUPS // 2 - 1) as k:
                for b in range(2):
                    store_group(2 * k + b, b)
                    load_group(2 * k + 2 + b, b, True)
            for b in range(2):
                store_group(GROUPS - 2 + b, b)
            for b in range(2):
                sp.wait_ge(out_out[b], 16 * (GROUPS // 2))

        @block.gpsimd
        def _(pool):
            nc.gpsimd.memset(pad_row[:, 0:C], 0.0).then_inc(pad_set, 1)
            nc.gpsimd.memset(pad_row[:, C:C + 1], OUT_OF_RANGE).then_inc(pad_set, 1)
            nc.gpsimd.memset(pad_row[:, C + 1:C + 2], -1.0).then_inc(pad_set, 1)
            nc.gpsimd.memset(ident[:], 0.0).then_inc(const_set, 1)
            nc.gpsimd.memset(ones[:], 1.0).then_inc(const_set, 1)
            pool.wait_ge(const_set, 2)
            nc.gpsimd.affine_select(out=ident[:], in_=ident[:], compare_op=ALU.not_equal, fill=1.0, base=0,
                                    pattern=[[-1, P]], channel_multiplier=1).then_inc(const_set, 1)
            nc.gpsimd.affine_select(out=before[:], in_=ones[:], compare_op=ALU.is_gt, fill=0.0, base=0,
                                    pattern=[[1, P]], channel_multiplier=-1).then_inc(const_set, 1)
            nc.gpsimd.iota(my_place[:], pattern=[[P, SORTED_TILES]], base=0, channel_multiplier=1,
                           allow_small_or_imprecise_dtypes=True).then_inc(const_set, 1)
            nc.gpsimd.iota(tile_no[:], pattern=[[1, SORTED_TILES]], base=0, channel_multiplier=0,
                           allow_small_or_imprecise_dtypes=True).then_inc(const_set, 1)
            pool.wait_ge(attn_hi_set, 1)
            nc.gpsimd.tensor_tensor(wa_lo[:], attn_stage, f32(wa_hi[:]), ALU.subtract).then_inc(attn_lo_set, 1)
            with pool.Fori(0, EXPERTS) as e:
                pool.wait_ge(experts_hi_set, e + 1)
                nc.gpsimd.tensor_tensor(wx_lo[:, ds(e, 1)], stage[:, ds(e, 1)],
                                        f32(wx_hi[:, ds(e, 1)]), ALU.subtract).then_inc(experts_lo_set, 1)

            def difference(g):
                b = g % 2
                pool.wait_ge(xt_set, 2 * g + 2)
                if g >= 2:
                    pool.wait_ge(mix_v_set, 2 * g - 2)
                if b == 1:
                    nc.gpsimd.tensor_copy(xt[1][:, :, 0:1], xt[0][:, :, GROUP:GROUP + 1]).then_inc(edge_set, 1)
                    pool.wait_ge(edge_set, g // 2 + 1)
                nc.gpsimd.tensor_tensor(diff[b].rearrange("p (k t) -> p k t", k=KC), xt[b][:, :, 1:GROUP + 1],
                                        xt[b][:, :, 0:GROUP], ALU.subtract).then_inc(diff_set, 1)

            def add_y(g):
                pool.wait_ge(scattered[g], 16 * TOPK * GT)
                pool.wait_ge(y_copied, 2 * g + 2)
                row = rows[:, g * GT:(g + 1) * GT, 0:C]
                nc.gpsimd.tensor_tensor(row, y_new.rearrange("p (t c) -> p t c", t=GT), row,
                                        ALU.add).then_inc(s_set, 1)

            pool.wait_ge(edge_zero, 1)
            difference(0)
            difference(1)
            pool.wait_ge(pads_out, 16)
            pool.wait_ge(places_set, 3)
            pool.wait_ge(rows_kept, GROUPS)
            for g in range(GROUPS):
                for t in range(g * GT, (g + 1) * GT):
                    for place in (place1, place2):
                        nc.gpsimd.indirect_dma_start(
                            sorted_rows, bass.IndirectOffsetOnAxis(ap=place[:, t:t + 1], axis=0),
                            rows[:, t, :], None).then_inc(scattered[g], 16)
                if 1 <= g < GROUPS - 1:
                    difference(g + 1)
                if g >= 1:
                    add_y(g - 1)
            add_y(GROUPS - 1)

            def scatter(i, r, first_half):
                pool.wait_ge(e_y_set[r % 2], first_half)
                pool.wait_ge(dest_set, i + 1)
                pool.sem_inc(scatter_ready, 1)
                nc.gpsimd.indirect_dma_start(
                    expert_rows, bass.IndirectOffsetOnAxis(ap=dest[:, r:r + 1], axis=0),
                    yring[:, r % YRING, :], None, bounds_check=last_row,
                    oob_is_err=False).then_inc(yring_out[r % YRING], 16)

            last_row = pool.to_reg(TOKENS * TOPK - 1)
            with pool.Fori(0, SORTED_TILES // XRING) as k:
                for r in range(XRING):
                    scatter(k * XRING + r, r, k * (XRING // 2) + r // 2 + 1)

        @block.scalar
        def _(act):
            act.dma_start(vec[:], vectors).then_inc(vec_in, 16)
            act.dma_start(bias_sb[:], bias).then_inc(vec_in, 16)
            act.dma_start(router_f[:], router).then_inc(router_in, 16)
            act.sem_inc(down_free, 1)
            for n in range(2):
                act.wait_ge(var_eps, n + 1)
                nc.scalar.activation(tmp_b[:], tmp_a[:], ACT.Sqrt).then_inc(root_set, 1)
            def t_hi(g, b):
                act.wait_ge(t_done, g + 1)
                nc.scalar.copy(in_hi[:, b, :], bank[:, 0:2, :]).then_inc(thi_set, 1)

            def shared_group(g, b, first_, last_):
                if not last_:
                    if not first_:
                        act.wait_ge(logit_done, g)
                        act.wait_ge(up_done, g)
                    t_hi(g + 1, 1 - b)
                act.wait_ge(xn_set, g * GT + GT)
                nc.scalar.copy(rows[:, ds(g * GT, GT), 0:C], x_norm[:, b * GT:(b + 1) * GT, :]).then_inc(rows_kept, 1)
                act.wait_ge(gate_done, g + 1)
                if not first_:
                    act.wait_ge(h_set, g)
                nc.scalar.activation(silu_g, bank[:, 2, :], ACT.Silu).then_inc(silu_set, 1)
                if first_:
                    act.wait_ge(experts_in, 32)
                nc.scalar.copy(wx_hi[:, ds(g, 1)], stage[:, ds(g, 1)]).then_inc(experts_hi_set, 1)
                act.wait_ge(h_set, g + 1)
                nc.scalar.copy(mid_hi[:, b, :], h_shared).then_inc(hhi_set, 1)
                if not first_:
                    shared_store(g - 1)

            def shared_store(g):
                act.wait_ge(down_done, g + 1)
                act.wait_ge(attn_lo_set, 1)
                nc.scalar.copy(shared_out[:, ds(g * GT * C, GT * C)], bank[:, 5:7, :]).then_inc(down_free, 1)

            t_hi(0, 0)
            act.wait_ge(attn_in, 16)
            nc.scalar.copy(wa_hi[:], attn_stage).then_inc(attn_hi_set, 1)
            shared_group(0, 0, True, False)
            with act.Fori(0, (GROUPS - 2) // 2) as k:
                shared_group(2 * k + 1, 1, False, False)
                shared_group(2 * k + 2, 0, False, False)
            shared_group(GROUPS - 1, 1, False, True)
            shared_store(GROUPS - 1)

            act.wait_ge(logit_read, GROUPS)
            act.wait_ge(experts_lo_set, EXPERTS)
            nc.scalar.activation(route_tmp[1], logit, ACT.Sigmoid).then_inc(score_set, 1)
            act.wait_ge(vec_in, 32)
            nc.scalar.activation(decay[:], vec[:, v_decay, :], ACT.Sigmoid).then_inc(params_set, 1)
            nc.scalar.activation(first[:], vec[:, v_first, :], ACT.Exp).then_inc(params_set, 1)

            def set_z(g):
                for t in range(GT):
                    nc.scalar.mul(z[:, t, :], rows[:, g * GT + t, 0:C], rstd2[:, ds(g * GT + t, 1)]).then_inc(z_set, 1)

            def set_xt(g, b):
                act.wait_ge(zt_done, g + 1)
                for k in range(KC):
                    nc.scalar.activation(xt[b][:, k, 1:GROUP + 1], bank[:, k, :], ACT.Identity,
                                         bias=vec[:, ln_b, k:k + 1], scale=vec[:, ln_w, k:k + 1]).then_inc(xt_set, 1)

            def k_hi(g):
                act.wait_ge(mix_k_set, 2 * g + 2)
                nc.scalar.copy(in_hi[:, 0, :], mix_k).then_inc(k_hi_set, 1)

            def rwkv_hi(g):
                for k in range(KC):
                    act.wait_ge(rwkv_set, 2 * g + k + 1)
                    nc.scalar.copy(mid_hi[:, k, :], rwkv[:, k * GROUP:(k + 1) * GROUP]).then_inc(rwhi_set, 1)

            def gate_r(g, k):
                act.wait_ge(r_done, 2 * g + k + 1)
                nc.scalar.activation(r_gate[:, k * GROUP:(k + 1) * GROUP], bank[:, 6, :],
                                     ACT.Sigmoid).then_inc(r_set, 1)

            def copy_y(g, pair, first_):
                act.wait_ge(y_done, 2 * g + pair + 1)
                if pair == 0 and not first_:
                    act.wait_ge(s_set, g)
                nc.scalar.copy(y_new[:, pair * GROUP:(pair + 1) * GROUP],
                               bank[:, 7 if pair == 0 else 0, :]).then_inc(y_copied, 1)

            def mix_group(g, b, before_=True, before2=True, after1=True, after2=True):
                if after1:
                    if before_:
                        act.wait_ge(mix_v_set, 2 * g)
                    set_xt(g + 1, 1 - b)
                if before_:
                    rwkv_hi(g - 1)
                if after2:
                    set_z(g + 2)
                gate_r(g, 0)
                if before_:
                    copy_y(g - 1, 0, not before2)
                gate_r(g, 1)
                if after1:
                    act.wait_ge(k_done, g + 1)
                    k_hi(g + 1)
                if before_:
                    copy_y(g - 1, 1, not before2)

            act.wait_ge(rstd2_set, 1)
            act.wait_ge(rows_kept, GROUPS)
            set_z(0)
            set_xt(0, 0)
            act.wait_ge(zt_done, 1)
            set_z(1)
            act.wait_ge(logit_done, GROUPS)
            k_hi(0)
            mix_group(0, 0, before_=False, before2=False)
            mix_group(1, 1, before2=False)
            with act.Fori(0, (GROUPS - 4) // 2) as k:
                mix_group(2 * k + 2, 0)
                mix_group(2 * k + 3, 1)
            mix_group(GROUPS - 2, 0, after2=False)
            mix_group(GROUPS - 1, 1, after1=False, after2=False)
            rwkv_hi(GROUPS - 1)
            for pair in range(2):
                copy_y(GROUPS - 1, pair, False)

            def step(s, u, half, peeled=False):
                def has(d):
                    return not peeled or 0 <= s - d < SORTED_TILES
                if has(0):
                    act.wait_ge(e_t_done, s + 1)
                    if has(2) :
                        act.wait_ge(e_gu_done, s - 1)
                    nc.scalar.copy(in_hi[:, u % 2, 0:C], bank[:, u % 2, 0:C]).then_inc(e_hi_set, 1)
                if has(1):
                    act.wait_ge(e_gu_done, s)
                    if has(3):
                        act.wait_ge(e_h_set, s - 2)
                    nc.scalar.activation(silu_t[:, (u - 1) % 2, :], bank[:, 2 + (u - 1) % 2, 0:INNER],
                                         ACT.Silu).then_inc(e_silu_set, 1)
                if has(2):
                    act.wait_ge(e_ht_done, s - 1)
                    if has(4):
                        act.wait_ge(e_down_done, s - 3)
                    nc.scalar.copy(mid_hi[:, u % 2, 0:INNER], bank[:, 4 + u % 2, 0:INNER]).then_inc(e_hhi_set, 1)
                if has(3) and (u - 3) % 2 == 0:
                    act.wait_ge(e_down_done, s - 2)
                    if has(3 + YRING):
                        act.wait_ge(yring_out[(u - 3) % YRING], 2 * (s - 3 - (u - 3) % YRING))
                    nc.scalar.copy(yring[:, (u - 3) % YRING, :], bank[:, 6, 0:C]).then_inc(e_y_set[0], 1)

            act.wait_ge(v_done, 2 * GROUPS)
            run_steps(act, step)

            def gate_group(g, b):
                act.wait_ge(y_in[b], 16 * g + 32 - 16 * b)
                for t in range(GT):
                    nc.scalar.mul(y_pair[:, b, t, 0:C], y_pair[:, b, t, 0:C],
                                  weight1[:, ds(g * GT + t, 1)]).then_inc(part_set, 1)
                act.wait_ge(sum_set, g + 1)
                nc.scalar.activation(acc, acc, ACT.Silu).then_inc(silu_y_set, 1)

            with act.Fori(0, GROUPS // 2) as k:
                for b in range(2):
                    gate_group(2 * k + b, b)

        def route(dve, link):
            def et(n):
                return route_tmp[n].rearrange("p (e t) -> p e t", e=EXPERTS)

            scores, choice, best = et(1), et(2), et(3)
            half = EXPERTS // 2
            dve.wait_ge(score_set, 1)
            dve.wait_ge(vec_in, 32)
            link(nc.vector.tensor_tensor(choice, scores, bias_sb[:].unsqueeze(2).to_broadcast([P, EXPERTS, TILES]), ALU.add))
            pairs = route_tmp[2].rearrange("p (h a t) -> p h a t", h=EXPERTS // 2, a=2)
            more = route_tmp[4].rearrange("p (h t) -> p h t", h=8)[:, 0:4]
            less = route_tmp[4].rearrange("p (h t) -> p h t", h=8)[:, 4:8]
            link(nc.vector.tensor_tensor(more, pairs[:, :, 0], pairs[:, :, 1], ALU.max))
            link(nc.vector.tensor_tensor(less, pairs[:, :, 0], pairs[:, :, 1], ALU.min))
            more2 = more.rearrange("p (n a) t -> p n a t", n=2)
            less2 = less.rearrange("p (n a) t -> p n a t", n=2)
            w = route_tmp[5].rearrange("p (x n t) -> p x n t", x=4, n=2)
            link(nc.vector.tensor_tensor(w[:, 0], more2[:, :, 0], more2[:, :, 1], ALU.max))
            link(nc.vector.tensor_tensor(w[:, 1], more2[:, :, 0], more2[:, :, 1], ALU.min))
            link(nc.vector.tensor_tensor(w[:, 2], less2[:, :, 0], less2[:, :, 1], ALU.max))
            link(nc.vector.tensor_tensor(w[:, 1], w[:, 1], w[:, 2], ALU.max))
            link(nc.vector.tensor_tensor(w[:, 0], w[:, 0], w[:, 1], ALU.add))
            link(nc.vector.tensor_tensor(w[:, 3, 1], w[:, 0, 1], w[:, 0, 0], ALU.is_gt))
            link(nc.vector.tensor_scalar(w[:, 3, 0], w[:, 3, 1], -1.0, 1.0, ALU.mult, ALU.add))
            for n in range(2):
                part = slice(n * half, (n + 1) * half)
                link(nc.vector.tensor_tensor(best[:, part], choice[:, part],
                                             w[:, 3, n].unsqueeze(1).to_broadcast([P, half, TILES]), ALU.mult))
            prefer = et(6)
            for e in range(EXPERTS):
                ins = nc.vector.memset(prefer[:, e, :], float(EXPERTS - e))
            link(ins)
            small = route_tmp[7].rearrange("p (x t) -> p x t", x=8)
            is_one, tmp = (et(8), et(9)), et(10)
            for n in range(TOPK):
                top = small[:, 0]
                link(nc.vector.tensor_reduce(top, best.rearrange("p e t -> p t e"), AX.X, ALU.max))
                link(nc.vector.tensor_tensor(tmp, best, top.unsqueeze(1).to_broadcast([P, EXPERTS, TILES]), ALU.is_equal))
                link(nc.vector.tensor_tensor(tmp, tmp, prefer, ALU.mult))
                link(nc.vector.tensor_reduce(top, tmp.rearrange("p e t -> p t e"), AX.X, ALU.max))
                link(nc.vector.tensor_tensor(is_one[n], tmp, top.unsqueeze(1).to_broadcast([P, EXPERTS, TILES]), ALU.is_equal))
                if n == 0:
                    link(nc.vector.scalar_tensor_tensor(best, is_one[0], REMOVED, best, ALU.mult, ALU.add))
            chosen = route_tmp[11].bitcast(BF16)[:, 0:ET]
            nc.vector.tensor_tensor(chosen, route_tmp[8], route_tmp[9], ALU.add).then_inc(chosen_set, 1)
            for n in range(TOPK):
                link(nc.vector.tensor_tensor(tmp, is_one[n], scores, ALU.mult))
                link(nc.vector.tensor_reduce(small[:, 1 + n], tmp.rearrange("p e t -> p t e"), AX.X, ALU.add))
            link(nc.vector.tensor_tensor(small[:, 3], small[:, 1], small[:, 2], ALU.add))
            link(nc.vector.tensor_scalar(small[:, 3], small[:, 3], 1e-20, None, ALU.add))
            link(nc.vector.reciprocal(small[:, 4], small[:, 3]))
            nc.vector.tensor_tensor(weight1[:], small[:, 1], small[:, 4], ALU.mult)
            nc.vector.tensor_tensor(weight2[:], small[:, 2], small[:, 4], ALU.mult)
            keep = et(12)
            nc.vector.memset(keep[:, :, 1:TILES], 1.0)
            link(nc.vector.memset(keep[:, :, 0:1], 0.0))
            dve.wait_ge(counted, 1)
            within, total = bank[:, 7, 0:ET], bank[:, 7, ET:2 * ET]
            link(nc.vector.tensor_tensor_scan(route_tmp[13], route_tmp[12], total, 0.0, ALU.mult, ALU.add))
            cnt = small[:, 5, 0:EXPERTS]
            tiles = small[:, 6, 0:EXPERTS]
            ends = small[:, 6, EXPERTS:2 * EXPERTS]
            starts = small[:, 6, 2 * EXPERTS:3 * EXPERTS]
            one8 = small[:, 5, EXPERTS:2 * EXPERTS]
            nc.vector.memset(one8, 1.0)
            link(nc.vector.tensor_scalar(int_tmp[:, 0:EXPERTS], et(13)[:, :, TILES - 1], float(P - 1), None, ALU.add))
            link(nc.vector.tensor_scalar(int_tmp[:, 0:EXPERTS], int_tmp[:, 0:EXPERTS], 7, None, ALU.logical_shift_right))
            link(nc.vector.tensor_copy(tiles, int_tmp[:, 0:EXPERTS]))
            link(nc.vector.tensor_tensor_scan(ends, one8, tiles, 0.0, ALU.mult, ALU.add))
            link(nc.vector.tensor_tensor(starts, ends, tiles, ALU.subtract))
            link(nc.vector.tensor_scalar(starts, starts, float(P), None, ALU.mult))
            place = et(13)
            link(nc.vector.tensor_tensor(route_tmp[13], route_tmp[13], total, ALU.subtract))
            link(nc.vector.tensor_tensor(route_tmp[13], within, route_tmp[13], ALU.add))
            link(nc.vector.tensor_tensor(place, place, starts.unsqueeze(2).to_broadcast([P, EXPERTS, TILES]), ALU.add))
            for n, to in enumerate((place1, place2)):
                link(nc.vector.tensor_tensor(tmp, is_one[n], place, ALU.mult))
                link(nc.vector.tensor_reduce(small[:, 1 + n], tmp.rearrange("p e t -> p t e"), AX.X, ALU.add))
                nc.vector.tensor_copy(to[:], small[:, 1 + n]).then_inc(places_set, 1)
            nc.vector.tensor_copy(rows[:, :, C + 1], small[:, 2])
            nc.vector.tensor_scalar(rows[:, :, C], my_place[:, 0:TILES], 2.0, None, ALU.mult).then_inc(places_set, 1)
            after = route_tmp[14].rearrange("p (e t) -> p e t", e=EXPERTS)
            for lo in (0, 32, 64):
                n = min(32, SORTED_TILES - lo)
                link(nc.vector.tensor_tensor(after[:, :, 0:n], tile_no[:, lo:lo + n].unsqueeze(1).to_broadcast([P, EXPERTS, n]),
                                             ends.unsqueeze(2).to_broadcast([P, EXPERTS, n]), ALU.is_ge))
                link(nc.vector.tensor_reduce(small[:, 7, 0:n], after[:, :, 0:n].rearrange("p e t -> p t e"), AX.X, ALU.add))
                link(nc.vector.tensor_scalar(weight_at[:, lo:lo + n], small[:, 7, 0:n], float(EXPERTS - 1), float(EW),
                                             ALU.min, ALU.mult))
            dve.sem_inc(places_set, 1)

        @block.vector
        def _(dve):
            steps = [0]

            def link(ins):
                steps[0] += 1
                ins.then_inc(dve_step, 1)
                dve.wait_ge(dve_step, steps[0])

            dve.wait_ge(router_in, 16)
            link(nc.vector.tensor_copy(wr_hi[:], router_f[:]))
            nc.vector.tensor_tensor(wr_lo[:], router_f[:], f32(wr_hi[:]), ALU.subtract).then_inc(shared_w_set, 1)

            for c in range(4):
                n = TILES // 4
                dve.wait_ge(x_in[c], 16)
                with dve.Fori(c * n, (c + 1) * n) as t:
                    nc.vector.bn_stats(stats[:, t, :], rows[:, t, 0:C]).then_inc(norm_set, 1)
            dve.wait_ge(norm_set, TILES)
            link(nc.vector.tensor_tensor(tmp_a[:], stats[:, :, 1], stats[:, :, 4], ALU.add))
            link(nc.vector.tensor_scalar(mean[:], tmp_a[:], 0.5, None, ALU.mult))
            link(nc.vector.tensor_tensor(tmp_a[:], stats[:, :, 1], stats[:, :, 4], ALU.subtract))
            link(nc.vector.tensor_tensor(tmp_a[:], tmp_a[:], tmp_a[:], ALU.mult))
            link(nc.vector.tensor_scalar(tmp_a[:], tmp_a[:], 0.25, None, ALU.mult))
            link(nc.vector.tensor_tensor(tmp_b[:], stats[:, :, 2], stats[:, :, 5], ALU.add))
            link(nc.vector.scalar_tensor_tensor(var[:], tmp_b[:], 1.0 / C, tmp_a[:], ALU.mult, ALU.add))

            def inverse_root(to, n):
                dve.wait_ge(root_set, n)
                link(nc.vector.reciprocal(to[:], tmp_b[:]))
                link(nc.vector.tensor_tensor(tmp_b[:], to[:], to[:], ALU.mult))
                link(nc.vector.tensor_tensor(tmp_b[:], tmp_b[:], tmp_a[:], ALU.mult))
                link(nc.vector.tensor_scalar(tmp_b[:], tmp_b[:], -0.5, 1.5, ALU.mult, ALU.add))
                link(nc.vector.tensor_tensor(to[:], to[:], tmp_b[:], ALU.mult))

            nc.vector.tensor_scalar(tmp_a[:], var[:], LN_EPS, None, ALU.add).then_inc(var_eps, 1)
            inverse_root(rstd, 1)
            link(nc.vector.tensor_tensor(tmp_a[:], var[:], rstd[:], ALU.mult))
            link(nc.vector.tensor_tensor(tmp_a[:], tmp_a[:], rstd[:], ALU.mult))
            link(nc.vector.tensor_scalar(tmp_a[:], tmp_a[:], LN_EPS, None, ALU.add))

            def set_xn(g, b, tiles=range(GT), reused=True):
                if reused:
                    dve.wait_ge(t_done, g - 1)
                    dve.wait_ge(rows_kept, g - 1)
                for t in tiles:
                    nc.vector.tensor_scalar(x_norm[:, b * GT + t, :], rows[:, g * GT + t, 0:C],
                                            mean[:, ds(g * GT + t, 1)], rstd[:, ds(g * GT + t, 1)],
                                            ALU.subtract, ALU.mult).then_inc(xn_set, 1)

            def t_lo(g, b):
                dve.wait_ge(thi_set, g + 1)
                nc.vector.tensor_tensor(in_lo[:, b, :], bank[:, 0:2, :].rearrange("p a c -> p (a c)"),
                                        f32(in_hi[:, b, :]), ALU.subtract).then_inc(tlo_set, 1)

            def shared_group(g, b, first_, last_, xn_ahead=True):
                if not last_:
                    if not first_:
                        dve.wait_ge(logit_done, g)
                        dve.wait_ge(up_done, g)
                    t_lo(g + 1, 1 - b)
                if xn_ahead:
                    set_xn(g + 2, b, range(0, GT // 2))
                dve.wait_ge(silu_set, g + 1)
                dve.wait_ge(up_done, g + 1)
                if not first_:
                    dve.wait_ge(hlo_set, g)
                nc.vector.tensor_tensor(h_shared, bank[:, 3, :], silu_g, ALU.mult).then_inc(h_set, 1)
                if xn_ahead:
                    set_xn(g + 2, b, range(GT // 2, GT))
                dve.wait_ge(hhi_set, g + 1)
                if not first_:
                    dve.wait_ge(down_done, g)
                nc.vector.tensor_tensor(mid_lo[:, b, :], h_shared, f32(mid_hi[:, b, :]),
                                        ALU.subtract).then_inc(hlo_set, 1)
                dve.wait_ge(logit_done, g + 1)
                nc.vector.tensor_copy(
                    logit.rearrange("p (e t) -> p e t", e=EXPERTS)[:, :, ds(g * GT, GT)],
                    bank[:, 4, 0:GT * EXPERTS].rearrange("p (t e) -> p e t", e=EXPERTS)).then_inc(logit_read, 1)

            set_xn(0, 0, reused=False)
            set_xn(1, 1, reused=False)
            dve.sem_inc(var_eps, 1)
            inverse_root(rstd2, 2)
            dve.sem_inc(rstd2_set, 1)
            dve.wait_ge(shared_in, 16)
            link(nc.vector.tensor_copy(wx_hi[:, SHARED], stage[:, SHARED]))
            nc.vector.tensor_tensor(wx_lo[:, SHARED], stage[:, SHARED], f32(wx_hi[:, SHARED]),
                                    ALU.subtract).then_inc(shared_w_set, 1)
            t_lo(0, 0)
            shared_group(0, 0, True, False)
            with dve.Fori(0, (GROUPS - 4) // 2) as k:
                shared_group(2 * k + 1, 1, False, False)
                shared_group(2 * k + 2, 0, False, False)
            shared_group(GROUPS - 3, 1, False, False)
            shared_group(GROUPS - 2, 0, False, False, xn_ahead=False)
            shared_group(GROUPS - 1, 1, False, True, xn_ahead=False)

            dve.wait_ge(experts_lo_set, EXPERTS)
            nc.vector.memset(xt[0][:, :, 0:1], 0.0).then_inc(edge_zero, 1)
            route(dve, link)

            dve.wait_ge(params_set, 2)

            def mixture(to, done, which, g, b):
                for k in range(KC):
                    cols = slice(k * GROUP, (k + 1) * GROUP)
                    nc.vector.scalar_tensor_tensor(to[:, cols], diff[b][:, cols], vec[:, which, k:k + 1],
                                                   xt[b][:, k, 0:GROUP], ALU.mult, ALU.add).then_inc(done, 1)

            def k_lo(g):
                dve.wait_ge(k_hi_set, g + 1)
                nc.vector.tensor_tensor(in_lo[:, 0, :], mix_k, f32(in_hi[:, 0, :]),
                                        ALU.subtract).then_inc(k_lo_set, 1)

            def finish_rwkv(g):
                for k in range(KC):
                    dve.wait_ge(k_read, 2 * g + k + 1)
                    dve.wait_ge(v_done, 2 * g + k + 1)
                    cols = slice(k * GROUP, (k + 1) * GROUP)
                    nc.vector.tensor_tensor(rwkv[:, cols], rwkv[:, cols], bank[:, 4 + k, :],
                                            ALU.mult).then_inc(v_read, 1)
                for k in range(KC):
                    dve.wait_ge(v_read, 2 * g + k + 1)
                    dve.wait_ge(r_set, 2 * g + k + 1)
                    cols = slice(k * GROUP, (k + 1) * GROUP)
                    nc.vector.tensor_tensor(rwkv[:, cols], rwkv[:, cols], r_gate[:, cols],
                                            ALU.mult).then_inc(rwkv_set, 1)
                for k in range(KC):
                    dve.wait_ge(rwhi_set, 2 * g + k + 1)
                    nc.vector.tensor_tensor(mid_lo[:, k, :], rwkv[:, k * GROUP:(k + 1) * GROUP],
                                            f32(mid_hi[:, k, :]), ALU.subtract).then_inc(rwlo_set, 1)

            def scan(g, b, before_):
                if before_:
                    dve.wait_ge(rwlo_set, 2 * g)
                dve.wait_ge(k_done, g + 1)
                for k in range(KC):
                    cols = slice(k * GROUP, (k + 1) * GROUP)
                    nc.vector.tensor_tensor_scan(rwkv[:, cols], decay[:, k:k + 1].to_broadcast([P, GROUP]),
                                                 bank[:, 2 + k, :], 0.0 if b == 0 else last_s[:, k:k + 1],
                                                 ALU.mult, ALU.add).then_inc(scan_set, 1)
                dve.wait_ge(scan_set, 2 * g + 2)
                nc.vector.tensor_copy(last_s[:], rwkv.rearrange("p (k t) -> p k t", k=KC)[:, :, GROUP - 1]).then_inc(last_set, 1)
                dve.wait_ge(last_set, g + 1)
                for k in range(KC):
                    cols = slice(k * GROUP, (k + 1) * GROUP)
                    nc.vector.scalar_tensor_tensor(rwkv[:, cols], rwkv[:, cols], first[:, k:k + 1],
                                                   bank[:, 2 + k, :], ALU.mult, ALU.add).then_inc(k_read, 1)

            def mix_group(g, b, before_=True, after1=True):
                if before_:
                    finish_rwkv(g - 1)
                scan(g, b, before_)
                mixture(mix_v, mix_v_set, mv, g, b)
                if after1:
                    dve.wait_ge(diff_set, g + 2)
                    mixture(mix_k, mix_k_set, mk, g + 1, 1 - b)
                    dve.wait_ge(r_done, 2 * g + 2)
                    mixture(mix_r, mix_r_set, mr, g + 1, 1 - b)
                    k_lo(g + 1)

            dve.wait_ge(diff_set, 1)
            mixture(mix_k, mix_k_set, mk, 0, 0)
            mixture(mix_r, mix_r_set, mr, 0, 0)
            k_lo(0)
            mix_group(0, 0, before_=False)
            with dve.Fori(0, (GROUPS - 2) // 2) as k:
                mix_group(2 * k + 1, 1)
                mix_group(2 * k + 2, 0)
            mix_group(GROUPS - 1, 1, after1=False)
            finish_rwkv(GROUPS - 1)

            def step(s, u, half, peeled=False):
                def has(d):
                    return not peeled or 0 <= s - d < SORTED_TILES
                if has(0):
                    dve.wait_ge(e_hi_set, s + 1)
                    nc.vector.tensor_tensor(in_lo[:, u % 2, 0:C], bank[:, u % 2, 0:C], f32(in_hi[:, u % 2, 0:C]),
                                            ALU.subtract).then_inc(e_lo_set, 1)
                if has(1):
                    dve.wait_ge(e_silu_set, s)
                    if has(3):
                        dve.wait_ge(e_ht_done, s - 2)
                    nc.vector.tensor_tensor(h_t[:, (u - 1) % 2, :], bank[:, 2 + (u - 1) % 2, INNER:2 * INNER],
                                            silu_t[:, (u - 1) % 2, :], ALU.mult).then_inc(e_h_set, 1)
                if has(2):
                    dve.wait_ge(e_hhi_set, s - 1)
                    nc.vector.tensor_tensor(mid_lo[:, u % 2, 0:INNER], bank[:, 4 + u % 2, 0:INNER],
                                            f32(mid_hi[:, u % 2, 0:INNER]), ALU.subtract).then_inc(e_hlo_set, 1)
                if has(3):
                    slot = (u - 3) % XRING
                    dve.wait_ge(xring_in[slot], 2 * (s - 3) + 16 - 2 * slot)
                    if has(3 + XRING):
                        dve.wait_ge(yring_out[slot], 2 * (s - 3 - slot))
                    nc.vector.scalar_tensor_tensor(dest[:, slot:slot + 1], xring[:, slot, C + 1:C + 2],
                                                   my_place[:, ds(s - 3, 1)], xring[:, slot, C:C + 1],
                                                   ALU.is_equal, ALU.add).then_inc(dest_set, 1)
                if has(3) and (u - 3) % 2 == 1:
                    dve.wait_ge(e_down_done, s - 2)
                    nc.vector.tensor_copy(yring[:, (u - 3) % YRING, :], bank[:, 7, 0:C]).then_inc(e_y_set[1], 1)

            run_steps(dve, step)

            def gate_group(g, b):
                for t in range(GT):
                    dve.wait_ge(part_set, g * GT + t + 1)
                    nc.vector.scalar_tensor_tensor(acc[:, t, :], y_pair[:, b, t, C:2 * C],
                                                   weight2[:, ds(g * GT + t, 1)], y_pair[:, b, t, 0:C],
                                                   ALU.mult, ALU.add).then_inc(routed_set, 1)
                dve.wait_ge(routed_set, g * GT + GT)
                flat = acc.rearrange("p t c -> p (t c)")
                nc.vector.tensor_tensor(flat, flat, shared_out[:, ds(g * GT * C, GT * C)], ALU.add).then_inc(sum_set, 1)
                dve.wait_ge(silu_y_set, g + 1)
                nc.vector.tensor_tensor(acc, acc, rows[:, ds(g * GT, GT), 0:C], ALU.mult).then_inc(gated_set, 1)
                dve.wait_ge(gated_set, g + 1)
                nc.vector.tensor_tensor(x_again[:, b], x_again[:, b], acc, ALU.add).then_inc(out_set, 1)
                dve.wait_ge(out_set, g + 1)

            dve.wait_ge(s_set, GROUPS)
            with dve.Fori(0, GROUPS // 2) as k:
                for b in range(2):
                    gate_group(2 * k + b, b)

        @block.tensor
        def _(pe):
            pe.wait_ge(const_set, 6)

            def product(out_ap, hi_l, lo_l, hi_r, lo_r, first_, last_, lolo=False):
                nc.tensor.matmul(out_ap, hi_l, hi_r, start=first_, stop=False)
                nc.tensor.matmul(out_ap, hi_l, lo_r, start=False, stop=False)
                if lolo:
                    nc.tensor.matmul(out_ap, lo_l, lo_r, start=False, stop=False)
                return nc.tensor.matmul(out_ap, lo_l, hi_r, start=False, stop=last_)

            def transposes(g, b):
                pe.wait_ge(xn_set, GT * (g + 1))
                for k in range(KC):
                    for t in range(GT):
                        mm = nc.tensor.transpose(bank[:, k, t * P:(t + 1) * P],
                                                 x_norm[:, b * GT + t, k * P:(k + 1) * P], ident[:])
                mm.then_inc(t_done, 1)

            def gate_up(g, b):
                pe.wait_ge(thi_set, g + 1)
                pe.wait_ge(tlo_set, g + 1)
                for n, done in ((0, gate_done), (1, up_done)):
                    for k in range(KC):
                        cols = slice((2 * k + n) * INNER, (2 * k + n + 1) * INNER)
                        tok = slice(k * GROUP, (k + 1) * GROUP)
                        mm = product(bank[:, 2 + n, :], wx_hi[:, SHARED, cols], wx_lo[:, SHARED, cols],
                                     in_hi[:, b, tok], in_lo[:, b, tok], k == 0, k == KC - 1)
                    mm.then_inc(done, 1)

            def down(g, b):
                pe.wait_ge(hhi_set, g + 1)
                pe.wait_ge(hlo_set, g + 1)
                pe.wait_ge(down_free, g + 1)
                for t in range(GT):
                    tok = slice(t * P, (t + 1) * P)
                    mm = product(bank[:, 5 + t // 2, (t % 2) * C:(t % 2 + 1) * C],
                                 mid_hi[:, b, tok], mid_lo[:, b, tok],
                                 wx_hi[:, SHARED, EW - C:EW], wx_lo[:, SHARED, EW - C:EW], True, True)
                mm.then_inc(down_done, 1)

            def logits(g, b, first_):
                if not first_:
                    pe.wait_ge(logit_read, g)
                for t in range(GT):
                    for k in range(KC):
                        tok = slice(k * GROUP + t * P, k * GROUP + (t + 1) * P)
                        mm = product(bank[:, 4, t * EXPERTS:(t + 1) * EXPERTS], in_hi[:, b, tok], in_lo[:, b, tok],
                                     wr_hi[:, k, :], wr_lo[:, k, :], k == 0, k == KC - 1, lolo=True)
                mm.then_inc(logit_done, 1)

            def shared_group(g, b, first_, last_):
                if not last_:
                    pe.wait_ge(thi_set, g + 1)
                    pe.wait_ge(tlo_set, g + 1)
                    transposes(g + 1, 1 - b)
                if not first_:
                    pe.wait_ge(silu_set, g)
                    pe.wait_ge(h_set, g)
                gate_up(g, b)
                if not first_:
                    down(g - 1, 1 - b)
                logits(g, b, first_)

            transposes(0, 0)
            pe.wait_ge(shared_w_set, 2)
            shared_group(0, 0, True, False)
            with pe.Fori(0, (GROUPS - 2) // 2) as k:
                shared_group(2 * k + 1, 1, False, False)
                shared_group(2 * k + 2, 0, False, False)
            shared_group(GROUPS - 1, 1, False, True)
            down(GROUPS - 1, 1)

            pe.wait_ge(chosen_set, 1)
            chosen = route_tmp[11].bitcast(BF16)[:, 0:ET]
            nc.tensor.matmul(bank[:, 7, 0:ET], before[:], chosen, start=True, stop=True)
            nc.tensor.matmul(bank[:, 7, ET:2 * ET], ones[:], chosen, start=True, stop=True).then_inc(counted, 1)

            def z_transposes(g):
                pe.wait_ge(z_set, GT * (g + 1))
                for k in range(KC):
                    for t in range(GT):
                        mm = nc.tensor.transpose(bank[:, k, t * P:(t + 1) * P], z[:, t, k * P:(k + 1) * P], ident[:])
                mm.then_inc(zt_done, 1)

            def project_k(d):
                for k in range(KC):
                    cols = slice(d * P, (d + 1) * P)
                    tok = slice(k * GROUP, (k + 1) * GROUP)
                    mm = product(bank[:, 2 + d, :], wa_hi[:, 0, k, cols], wa_lo[:, 0, k, cols],
                                 in_hi[:, 0, tok], in_lo[:, 0, tok], k == 0, k == KC - 1)
                return mm

            def project(w, d, bank_no, mixed):
                for k in range(KC):
                    mm = nc.tensor.matmul(bank[:, bank_no, :], wa[:, w, k, d * P:(d + 1) * P],
                                          mixed[:, k * GROUP:(k + 1) * GROUP], start=k == 0, stop=k == KC - 1)
                return mm

            def y_out(g, pair):
                for t in range(2):
                    for k in range(KC):
                        tok = slice((2 * pair + t) * P, (2 * pair + t + 1) * P)
                        mm = product(bank[:, 7 if pair == 0 else 0, t * C:(t + 1) * C],
                                     mid_hi[:, k, tok], mid_lo[:, k, tok],
                                     wa_hi[:, 1, k, :], wa_lo[:, 1, k, :], k == 0, k == KC - 1)
                mm.then_inc(y_done, 1)

            def mix_group(g, b, before_=True, before2=True, after1=True):
                if before2:
                    pe.wait_ge(y_copied, 2 * g - 2)
                if after1:
                    pe.wait_ge(xt_set, 2 * g + 2)
                    z_transposes(g + 1)
                pe.wait_ge(k_hi_set, g + 1)
                pe.wait_ge(k_lo_set, g + 1)
                if before_:
                    pe.wait_ge(k_read, 2 * g)
                for d in range(KC):
                    mm = project_k(d)
                mm.then_inc(k_done, 1)
                for d in range(KC):
                    pe.wait_ge(mix_r_set, 2 * g + 2)
                    if d == 1 or before_:
                        pe.wait_ge(r_set, 2 * g + d)
                    project(0, d, 6, mix_r).then_inc(r_done, 1)
                    if before_:
                        if d == 0:
                            pe.wait_ge(rwhi_set, 2 * g)
                            pe.wait_ge(rwlo_set, 2 * g)
                        elif after1:
                            pe.wait_ge(xt_set, 2 * g + 4)
                        y_out(g - 1, d)
                pe.wait_ge(mix_v_set, 2 * g + 2)
                if before_:
                    pe.wait_ge(v_read, 2 * g)
                for d in range(KC):
                    project(1, d, 4 + d, mix_v).then_inc(v_done, 1)

            z_transposes(0)
            pe.wait_ge(attn_lo_set, 1)
            pe.wait_ge(wa_in, 16)
            pe.wait_ge(logit_read, GROUPS)
            pe.wait_ge(down_free, GROUPS + 1)
            mix_group(0, 0, before_=False, before2=False)
            mix_group(1, 1, before2=False)
            with pe.Fori(0, (GROUPS - 4) // 2) as k:
                mix_group(2 * k + 2, 0)
                mix_group(2 * k + 3, 1)
            mix_group(GROUPS - 2, 0)
            mix_group(GROUPS - 1, 1, after1=False)
            pe.wait_ge(rwhi_set, 2 * GROUPS)
            pe.wait_ge(rwlo_set, 2 * GROUPS)
            pe.wait_ge(y_copied, 2 * GROUPS - 2)
            for pair in range(2):
                y_out(GROUPS - 1, pair)
            pe.wait_ge(y_copied, 2 * GROUPS)

            pe.wait_ge(places_set, 4)
            pe.wait_ge(experts_lo_set, EXPERTS)

            wx_hi_flat = wx_hi[:].rearrange("p e w -> p (e w)")
            wx_lo_flat = wx_lo[:].rearrange("p e w -> p (e w)")

            tile_regs = [pe.alloc_register(f"weights_of_{j}") for j in range(XRING + 2)]
            weights_of = {}

            def load_weights(tile, first_key, n):
                pe.load(tile_regs[0:n], weight_at[0:1, ds(tile, n)])
                weights_of.clear()
                for j in range(n):
                    weights_of[first_key + j] = pe.snap(tile_regs[j], min_val=0, max_val=(EXPERTS - 1) * EW)

            def step(s, u, half, peeled=False):
                def has(d):
                    return not peeled or 0 <= s - d < SORTED_TILES
                if has(0):
                    slot = u % XRING
                    pe.wait_ge(xring_in[slot], 2 * s + 16 - 2 * slot)
                    if has(2):
                        pe.wait_ge(e_lo_set, s - 1)
                    for k in range(KC):
                        mm = nc.tensor.transpose(bank[:, u % 2, k * P:(k + 1) * P],
                                                 xring[:, slot, k * P:(k + 1) * P], ident[:])
                    mm.then_inc(e_t_done, 1)
                if has(1):
                    v = weights_of[u - 1]
                    pe.wait_ge(e_lo_set, s)
                    if has(3):
                        pe.wait_ge(e_h_set, s - 2)
                    b = (u - 1) % 2
                    for k in range(KC):
                        tok = slice(k * P, (k + 1) * P)
                        mm = product(bank[:, 2 + b, 0:2 * INNER], in_hi[:, b, tok], in_lo[:, b, tok],
                                     wx_hi_flat[:, ds(v + k * 2 * INNER, 2 * INNER)],
                                     wx_lo_flat[:, ds(v + k * 2 * INNER, 2 * INNER)], k == 0, k == KC - 1)
                    mm.then_inc(e_gu_done, 1)
                if has(2):
                    pe.wait_ge(e_h_set, s - 1)
                    if has(4):
                        pe.wait_ge(e_hlo_set, s - 3)
                    nc.tensor.transpose(bank[:, 4 + u % 2, 0:P], h_t[:, u % 2, :], ident[:]).then_inc(e_ht_done, 1)
                if has(3):
                    v = weights_of[u - 3]
                    pe.wait_ge(e_hlo_set, s - 2)
                    b = (u - 3) % 2
                    if has(5):
                        pe.wait_ge(e_y_set[b], half)
                    product(bank[:, 6 + b, 0:C], mid_hi[:, b, 0:INNER], mid_lo[:, b, 0:INNER],
                            wx_hi_flat[:, ds(v + 2 * KC * INNER, C)],
                            wx_lo_flat[:, ds(v + 2 * KC * INNER, C)], True, True).then_inc(e_down_done, 1)

            run_steps(pe, step, load_weights)


def kernel(**inputs):
    import numpy as np
    import concourse.bacc as bacc
    from concourse.bass_utils import run_bass_kernel_spmd

    given = {name.removeprefix("L0_"): np.asarray(a) for name, a in inputs.items()}

    def chunks(a):
        return a.reshape(KC, P, -1).transpose(1, 0, 2)

    vectors = np.stack([given["attn_" + n].reshape(KC, P).T for n in
                        ("time_mix_k", "time_mix_v", "time_mix_r", "time_decay", "time_first", "ln_w", "ln_b")], 1)
    experts = [np.concatenate([given["ffn_w_" + n], given["ffn_sw_" + n][None]]) for n in ("gate", "up", "down")]
    gate_up = np.stack([w.reshape(EXPERTS + 1, KC, P, INNER) for w in experts[0:2]], 3).transpose(2, 0, 1, 3, 4)
    arrays = {
        "x": given["attn_x"],
        "vectors": vectors,
        "bias": np.broadcast_to(given["ffn_correction_bias"], (P, EXPERTS)),
        "router": chunks(given["ffn_router_weight"].T),
        "wk_wo": np.stack([chunks(given["attn_" + n].T) for n in ("Wk", "Wo")], 1),
        "wr_wv": np.stack([chunks(given["attn_" + n].T) for n in ("Wr", "Wv")], 1),
        "expert_w": np.concatenate([gate_up.reshape(P, EXPERTS + 1, -1), experts[2].transpose(1, 0, 2)], 2),
    }
    arrays = {name: np.ascontiguousarray(a) for name, a in arrays.items()}
    nc = bacc.Bacc("TRN2", target_bir_lowering=False, num_devices=1)
    args = [nc.dram_tensor(name, a.shape, F32, kind="ExternalInput").ap() for name, a in arrays.items()]
    out = nc.dram_tensor("out", (BATCH, SEQ, C), F32, kind="ExternalOutput").ap()
    gated_time_mix_kernel(nc, *args, out)
    result = run_bass_kernel_spmd(nc, [arrays], core_ids=[0])
    return result.results[0]["out"]
```

```python
from contextlib import ExitStack

import concourse.bass as bass
from concourse import mybir

F32 = mybir.dt.float32
F32R = mybir.dt.float32r
BF16 = mybir.dt.bfloat16
I32 = mybir.dt.int32
U32 = mybir.dt.uint32
ALU = mybir.AluOpType
ACT = mybir.ActivationFunctionType
AX = mybir.AxisListType
ds = bass.ds

P = 128
BATCH, SEQ, C = 4, 1024, 256
TOKENS = BATCH * SEQ
KC = C // P
EXPERTS, INNER, TOPK = 8, 128, 2
TILES = TOKENS // P
GROUP = 512
GT = GROUP // P
GROUPS = TOKENS // GROUP
ROW = C + 2
SORTED_TILES = TOKENS * TOPK // P + EXPERTS
SORTED_ROWS = SORTED_TILES * P
EW = 2 * KC * INNER + C
SHARED = EXPERTS
LN_EPS = 1e-5
OUT_OF_RANGE = float(TOKENS * TOPK)
REMOVED = -1e30
XRING, YRING = 8, 8

HEAD, UNROLL = 8, 16


def half_tiles(s):
    return (s - 5) // 2 + 1

def run_steps(eng, step, use_weights=None, after=None):
    if use_weights:
        use_weights(0, HEAD - 1)
    for s in range(HEAD):
        step(s, s, half_tiles(s), True)
        if after:
            after(s)
    with eng.Fori(0, (SORTED_TILES - HEAD) // UNROLL) as k:
        if use_weights:
            use_weights(HEAD - 3, UNROLL + 2)
        for u in range(HEAD, HEAD + UNROLL):
            step(k * UNROLL + u, u, k * (UNROLL // 2) + half_tiles(u))
    if use_weights:
        use_weights(SORTED_TILES - 3, 3)
    for s in range(SORTED_TILES, SORTED_TILES + 3):
        step(s, s, half_tiles(s), True)


def gated_time_mix_kernel(nc, x, vectors, bias, router, wk_wo, wr_wv, expert_w, out):
    sorted_rows = nc.dram_tensor("sorted_rows", [SORTED_ROWS, ROW], F32).ap()
    expert_rows = nc.dram_tensor("expert_rows", [TOKENS * TOPK, C], F32).ap()
    x_tiles = x.rearrange("b (j p) c -> p (b j) c", p=P)
    out_tiles = out.rearrange("b (j p) c -> p (b j) c", p=P)
    expert_tiles = expert_rows.rearrange("(j p k) c -> p j (k c)", p=P, k=TOPK)

    with ExitStack() as ctx:
        def sb(name, shape, dt=F32):
            return ctx.enter_context(nc.sbuf_tensor(name, shape, dt))

        def sem(name):
            return ctx.enter_context(nc.semaphore(name))

        rows = sb("rows", [P, TILES, ROW])
        shared_out = sb("shared_out", [P, TILES * C])
        wx_hi = sb("wx_hi", [P, EXPERTS + 1, EW], F32R)
        wx_lo = sb("wx_lo", [P, EXPERTS + 1, EW], F32R)
        wa_hi = sb("wa_hi", [P, 2, KC, C], F32R)
        wa_lo = sb("wa_lo", [P, 2, KC, C], F32R)
        wa = sb("wa", [P, 2, KC, C])
        wr = sb("wr", [P, KC, 2, EXPERTS], F32R)
        in_hi = sb("in_hi", [P, 2, KC * GROUP], F32R)
        in_lo = sb("in_lo", [P, 2, KC * GROUP], F32R)
        mid_hi = sb("mid_hi", [P, 2, GROUP], F32R)
        mid_lo = sb("mid_lo", [P, 2, GROUP], F32R)

        xring = sb("xring", [P, XRING, ROW])
        pad_row = sb("pad_row", [P, ROW])
        dest = sb("dest", [P, XRING], U32)
        vec = sb("vec", [P, 7, KC])
        mk, mv, mr, v_decay, v_first, ln_w, ln_b = range(7)
        bias_sb = sb("bias_sb", [P, EXPERTS])
        router_f = sb("router_f", [P, KC, EXPERTS])
        decay = sb("decay", [P, KC])
        first = sb("first", [P, KC])
        stats = sb("stats", [P, TILES, 6])
        mean = sb("mean", [P, TILES])
        var = sb("var", [P, TILES])
        rstd = sb("rstd", [P, TILES])
        rstd2 = sb("rstd2", [P, TILES])
        tmp_a = sb("tmp_a", [P, TILES])
        tmp_b = sb("tmp_b", [P, TILES])
        ident = sb("ident", [P, P])
        before = sb("before", [P, P], BF16)
        ones = sb("ones", [P, P], BF16)
        place1 = sb("place1", [P, TILES], U32)
        place2 = sb("place2", [P, TILES], U32)
        weight1 = sb("weight1", [P, TILES])
        weight2 = sb("weight2", [P, TILES])
        my_place = sb("my_place", [P, SORTED_TILES])
        tables = sb("tables", [P, 4, EXPERTS * TILES])
        prefer, keep = [tables[:, n].rearrange("p (e t) -> p e t", e=EXPERTS) for n in range(2)]
        extra = tables[:, 2:4]
        chosen_scores = sb("chosen_scores", [P, 3, TILES])
        weight_at = sb("weight_at", [P, SORTED_TILES + UNROLL], I32)
        int_tmp = sb("int_tmp", [P, EXPERTS], I32)
        last_s = sb("last_s", [P, KC])

        scratch = sb("scratch", [P, 8196])
        shared_end = TILES * C
        attn_stage = shared_out[:, shared_end - 2 * KC * C:shared_end].rearrange(
            "p (w k c) -> p w k c", w=2, k=KC)
        stage = scratch[:, 0:9 * EW].rearrange("p (e w) -> p e w", e=9)
        silu_g = scratch[:, 9 * EW:9 * EW + GROUP]
        h_shared = scratch[:, 9 * EW + GROUP:9 * EW + 2 * GROUP]
        GK = KC * GROUP
        z = scratch[:, 0:GK].rearrange("p (t c) -> p t c", t=GT)
        xt = [scratch[:, GK + h * KC * (GROUP + 1):GK + (h + 1) * KC * (GROUP + 1)].rearrange(
            "p (k t) -> p k t", k=KC) for h in range(2)]
        at = GK + 2 * KC * (GROUP + 1)
        diff = [scratch[:, at:at + GK], sb("diff_odd", [P, GK])[:]]
        mix_k = scratch[:, at + GK:at + 2 * GK]
        rwkv = scratch[:, at + 2 * GK:at + 3 * GK]
        y_new = scratch[:, at + 3 * GK:at + 4 * GK]
        r_gate = scratch[:, at + 4 * GK:at + 5 * GK]
        xring_flat = xring[:].rearrange("p r c -> p (r c)")
        mix_r = xring_flat[:, 0:GK]
        mix_v = xring_flat[:, XRING // 2 * ROW:XRING // 2 * ROW + GK]
        ET = EXPERTS * TILES
        rwkv_parts, y_parts, v_parts = [[a[:, n * ET:(n + 1) * ET] for n in range(4)] for a in (rwkv, y_new, mix_v)]
        route_tmp = {1: y_parts[0], 8: y_parts[1], 9: y_parts[2], 7: y_parts[3],
                     2: rwkv_parts[0], 3: rwkv_parts[1], 4: rwkv_parts[2], 5: rwkv_parts[3],
                     6: v_parts[0], 11: v_parts[1], 12: v_parts[2], 13: v_parts[3],
                     10: extra[:, 0], 14: extra[:, 1]}
        logit = scratch[:, 9 * EW + 2 * GROUP:9 * EW + 2 * GROUP + ET]
        logit_rows = diff[1][0:2 * EXPERTS, 0:GROUP]
        logit_low = extra[:, 0, 0:GT * EXPERTS].rearrange("p (e t) -> p e t", e=EXPERTS)
        silu_t = scratch[:, 7172:7172 + 2 * INNER].rearrange("p (b i) -> p b i", b=2)
        h_t = scratch[:, 7172 + 2 * INNER:7172 + 4 * INNER].rearrange("p (b i) -> p b i", b=2)
        yring = scratch[:, 0:YRING * C].rearrange("p (r c) -> p r c", r=YRING)
        X_LINEAR = 5
        x_again = scratch[:, YRING * C:YRING * C + X_LINEAR * GK].rearrange("p (g t c) -> p g t c", g=X_LINEAR, t=GT)
        x_of = [x_again[:, g] for g in range(X_LINEAR)] + [
            a.rearrange("p (t c) -> p t c", t=GT) for a in
            (diff[1], wa[:].rearrange("p w k c -> p (w k c)"), tables[:].rearrange("p a n -> p (a n)"))]
        y_slots = [w[:].rearrange("p e w -> p (e w)").bitcast(F32)[:, 0:6 * GK].rearrange(
            "p (n t c) -> p n t c", n=3, t=GT) for w in (wx_hi, wx_lo)]
        acc = [xring_flat[:, b * GK:(b + 1) * GK].rearrange("p (t c) -> p t c", t=GT) for b in range(2)]
        x_norm = xring[:, :, 0:C]

        bank = ctx.enter_context(nc.psum_tensor("bank", [P, 8, GROUP], F32))

        x_in = [sem(f"x_in{c}") for c in range(4)]
        rows_kept = sem("rows_kept")
        vec_in, router_in, shared_in = sem("vec_in"), sem("router_in"), sem("shared_in")
        attn_in, experts_in, wa_in = sem("attn_in"), sem("experts_in"), sem("wa_in")
        pads_out = sem("pads_out")
        scattered = [sem(f"scattered{g}") for g in range(GROUPS)]
        xring_in = [sem(f"xring_in{r}") for r in range(XRING)]
        yring_out = [sem(f"yring_out{r}") for r in range(YRING)]
        x_again_in = sem("x_again_in")
        y_in = [sem(f"y_in{n}") for n in range(6)]
        out_out = sem("out_out")
        pad_set, const_set, edge_zero = sem("pad_set"), sem("const_set"), sem("edge_zero")
        attn_hi_set, attn_lo_set = sem("attn_hi_set"), sem("attn_lo_set")
        experts_hi_set, experts_lo_set = sem("experts_hi_set"), sem("experts_lo_set")
        shared_hi_set, shared_w_set, params_set = sem("shared_hi_set"), sem("shared_w_set"), sem("params_set")
        dve_step = sem("dve_step")
        var_eps, root_set, norm_set = sem("var_eps"), sem("root_set"), sem("norm_set")
        rstd2_set = sem("rstd2_set")
        xn_set, t_done, thi_set, tlo_set = sem("xn_set"), sem("t_done"), sem("thi_set"), sem("tlo_set")
        gate_done, up_done, silu_set, h_set = sem("gate_done"), sem("up_done"), sem("silu_set"), sem("h_set")
        hhi_set, hlo_set, down_done, down_free = sem("hhi_set"), sem("hlo_set"), sem("down_done"), sem("down_free")
        logit_done, logit_kept = sem("logit_done"), sem("logit_kept")
        logit_turned, logit_read = sem("logit_turned"), sem("logit_read")
        turn_ready = sem("turn_ready")
        logit_low_set = sem("logit_low_set")
        score_set, chosen_set, counted, places_set = sem("score_set"), sem("chosen_set"), sem("counted"), sem("places_set")
        table_set, scores_read, column_set = sem("table_set"), sem("scores_read"), sem("column_set")
        column_turned, weight_at_set, pool_step = sem("column_turned"), sem("weight_at_set"), sem("pool_step")
        z_set, zt_done, xt_set = sem("z_set"), sem("zt_done"), sem("xt_set")
        edge_set, diff_set = sem("edge_set"), sem("diff_set")
        mix_k_set, mix_r_set, mix_v_set = sem("mix_k_set"), sem("mix_r_set"), sem("mix_v_set")
        k_hi_set, k_lo_set, k_done = sem("k_hi_set"), sem("k_lo_set"), sem("k_done")
        r_done, r_set, v_done = sem("r_done"), sem("r_set"), sem("v_done")
        scan_set, k_read, v_read, rwkv_set = sem("scan_set"), sem("k_read"), sem("v_read"), sem("rwkv_set")
        rwhi_set, rwlo_set, y_done = sem("rwhi_set"), sem("rwlo_set"), sem("y_done")
        last_set = sem("last_set")
        y_copied, s_set = sem("y_copied"), sem("s_set")
        e_t_done, e_hi_set, e_lo_set, e_gu_done = sem("e_t_done"), sem("e_hi_set"), sem("e_lo_set"), sem("e_gu_done")
        e_silu_set, e_h_set, e_ht_done = sem("e_silu_set"), sem("e_h_set"), sem("e_ht_done")
        e_hhi_set, e_hlo_set, e_down_done = sem("e_hhi_set"), sem("e_hlo_set"), sem("e_down_done")
        e_y_set = [sem("e_y_even_set"), sem("e_y_odd_set")]
        dest_set, scatter_ready = sem("dest_set"), sem("scatter_ready")
        part_set, routed_set, sum_set, silu_y_set = sem("part_set"), sem("routed_set"), sem("sum_set"), sem("silu_y_set")
        gated_set, out_set, last_out_set = sem("gated_set"), sem("out_set"), sem("last_out_set")
        gated_last_set = sem("gated_last_set")

        block = ctx.enter_context(nc.Block())

        def f32(ap):
            return ap.bitcast(F32)

        @block.sync
        def _(sp):
            for c in range(4):
                n = TILES // 4
                sp.dma_start(rows[:, c * n:(c + 1) * n, 0:C], x_tiles[:, c * n:(c + 1) * n, :]).then_inc(x_in[c], 16)
                if c == 0:
                    sp.dma_start(stage[:, SHARED], expert_w[:, SHARED]).then_inc(shared_in, 16)
            sp.dma_start(attn_stage, wk_wo).then_inc(attn_in, 16)
            for e in range(0, EXPERTS, 4):
                sp.dma_start(stage[:, e:e + 4], expert_w[:, e:e + 4]).then_inc(experts_in, 16)
            sp.dma_start(wa[:], wr_wv).then_inc(wa_in, 16)
            sp.wait_ge(pad_set, 3)
            sp.wait_ge(wa_in, 16)
            sp.dma_start(sorted_rows.rearrange("(i p) c -> p i c", p=P),
                         pad_row[:].unsqueeze(1).to_broadcast([P, SORTED_TILES, ROW])).then_inc(pads_out, 16)

            for g in range(GROUPS):
                sp.wait_ge(scattered[g], 16 * TOPK * GT)

            def load_sorted(i, slot, reused):
                if reused:
                    sp.wait_ge(e_t_done, i - XRING + 1)
                    sp.wait_ge(dest_set, i - XRING + 1)
                sp.dma_start(xring[:, slot, :], sorted_rows[ds(i * P, P), :]).then_inc(xring_in[slot], 16)

            sp.wait_ge(r_done, 2 * GROUPS)
            for r in range(XRING // 2):
                load_sorted(r, r, False)
            sp.wait_ge(v_done, 2 * GROUPS)
            for r in range(XRING // 2, XRING):
                load_sorted(r, r, False)
            with sp.Fori(0, X_LINEAR) as k:
                for r in range(XRING):
                    load_sorted(k * XRING + XRING + r, r, True)
                sp.wait_ge(s_set, GROUPS)
                sp.dma_start(x_again[:, ds(k, 1)].rearrange("p g t c -> p (g t) c"),
                             x_tiles[:, ds(k * GT, GT), :]).then_inc(x_again_in, 16)
            for k in range(X_LINEAR, GROUPS):
                for r in range(XRING):
                    load_sorted(k * XRING + XRING + r, r, True)
                sp.dma_start(x_of[k], x_tiles[:, k * GT:(k + 1) * GT, :]).then_inc(x_again_in, 16)

            for n in range(YRING):
                sp.wait_ge(yring_out[n], 16 * (SORTED_TILES // YRING))

            def load_y(g, b, n):
                sp.dma_start(y_slots[b][:, n], expert_tiles[:, ds(g * GT, GT), :]).then_inc(y_in[g % 6], 16)

            sp.wait_ge(e_down_done, SORTED_TILES)
            for g in range(6):
                load_y(g, g % 2, g // 2)
            for g in (6, 7):
                sp.wait_ge(routed_set, GT * (g - 5))
                load_y(g, g % 2, 0)
            for g in (0, 1, 2, 3, 4, 5, 7, 6):
                if g == GROUPS - 1:
                    sp.wait_ge(last_out_set, 1)
                else:
                    sp.wait_ge(out_set, g + 1)
                sp.dma_start(out_tiles[:, g * GT:(g + 1) * GT, :], x_of[g]).then_inc(out_out, 16)
            sp.wait_ge(out_out, 16 * GROUPS)

        @block.gpsimd
        def _(pool):
            nc.gpsimd.memset(pad_row[:, 0:C], 0.0).then_inc(pad_set, 1)
            nc.gpsimd.memset(pad_row[:, C:C + 1], OUT_OF_RANGE).then_inc(pad_set, 1)
            nc.gpsimd.memset(pad_row[:, C + 1:C + 2], -1.0).then_inc(pad_set, 1)
            nc.gpsimd.memset(ident[:], 0.0).then_inc(const_set, 1)
            nc.gpsimd.memset(ones[:], 1.0).then_inc(const_set, 1)
            pool.wait_ge(const_set, 2)
            nc.gpsimd.affine_select(out=ident[:], in_=ident[:], compare_op=ALU.not_equal, fill=1.0, base=0,
                                    pattern=[[-1, P]], channel_multiplier=1).then_inc(const_set, 1)
            nc.gpsimd.affine_select(out=before[:], in_=ones[:], compare_op=ALU.is_gt, fill=0.0, base=0,
                                    pattern=[[1, P]], channel_multiplier=-1).then_inc(const_set, 1)
            nc.gpsimd.iota(my_place[:], pattern=[[P, SORTED_TILES]], base=0, channel_multiplier=1,
                           allow_small_or_imprecise_dtypes=True).then_inc(const_set, 1)
            for e in range(EXPERTS):
                nc.gpsimd.memset(prefer[:, e, :], float(EXPERTS - e)).then_inc(table_set, 1)
            nc.gpsimd.memset(keep[:, :, 1:TILES], 1.0).then_inc(table_set, 1)
            nc.gpsimd.memset(keep[:, :, 0:1], 0.0).then_inc(table_set, 1)
            pool.wait_ge(shared_hi_set, 1)
            nc.gpsimd.tensor_tensor(wx_lo[:, SHARED], stage[:, SHARED], f32(wx_hi[:, SHARED]),
                                    ALU.subtract).then_inc(shared_w_set, 1)
            pool.wait_ge(attn_hi_set, 1)
            nc.gpsimd.tensor_tensor(wa_lo[:], attn_stage, f32(wa_hi[:]), ALU.subtract).then_inc(attn_lo_set, 1)
            with pool.Fori(0, EXPERTS) as e:
                pool.wait_ge(experts_hi_set, e + 1)
                nc.gpsimd.tensor_tensor(wx_lo[:, ds(e, 1)], stage[:, ds(e, 1)],
                                        f32(wx_hi[:, ds(e, 1)]), ALU.subtract).then_inc(experts_lo_set, 1)

            def difference(g):
                b = g % 2
                pool.wait_ge(xt_set, 2 * g + 2)
                if g >= 2:
                    pool.wait_ge(mix_v_set, 2 * g - 2)
                if b == 1:
                    nc.gpsimd.tensor_copy(xt[1][:, :, 0:1], xt[0][:, :, GROUP:GROUP + 1]).then_inc(edge_set, 1)
                    pool.wait_ge(edge_set, g // 2 + 1)
                nc.gpsimd.tensor_tensor(diff[b].rearrange("p (k t) -> p k t", k=KC), xt[b][:, :, 1:GROUP + 1],
                                        xt[b][:, :, 0:GROUP], ALU.subtract).then_inc(diff_set, 1)

            def add_y(g):
                pool.wait_ge(scattered[g], 16 * TOPK * GT)
                pool.wait_ge(y_copied, 2 * g + 2)
                row = rows[:, g * GT:(g + 1) * GT, 0:C]
                nc.gpsimd.tensor_tensor(row, y_new.rearrange("p (t c) -> p t c", t=GT), row,
                                        ALU.add).then_inc(s_set, 1)

            pool.wait_ge(edge_zero, 1)
            difference(0)

            pool.wait_ge(chosen_set, 1)
            product, steps = route_tmp[14], 0
            for n in range(TOPK):
                ins = nc.gpsimd.tensor_tensor(product, route_tmp[8 + n], route_tmp[1], ALU.mult)
                for width in (ET // 2, ET // 4, ET // 8):
                    steps += 1
                    ins.then_inc(pool_step, 1)
                    pool.wait_ge(pool_step, steps)
                    to = product[:, 0:width] if width > TILES else chosen_scores[:, n]
                    ins = nc.gpsimd.tensor_tensor(to, product[:, 0:width], product[:, width:2 * width], ALU.add)
                steps += 1
                ins.then_inc(pool_step, 1)
                pool.wait_ge(pool_step, steps)
            nc.gpsimd.tensor_tensor(chosen_scores[:, 2], chosen_scores[:, 0], chosen_scores[:, 1], ALU.add).then_inc(pool_step, 1)
            pool.wait_ge(pool_step, steps + 1)
            nc.gpsimd.tensor_scalar(chosen_scores[:, 2], chosen_scores[:, 2], 1e-20, None, ALU.add).then_inc(scores_read, 1)
            difference(1)
            pool.wait_ge(pads_out, 16)
            pool.wait_ge(places_set, 3)
            pool.wait_ge(rows_kept, GROUPS)
            for g in range(GROUPS):
                if g >= 2:
                    add_y(g - 2)
                if 1 <= g < GROUPS - 1:
                    difference(g + 1)
                for t in range(g * GT, (g + 1) * GT):
                    for place in (place1, place2):
                        nc.gpsimd.indirect_dma_start(
                            sorted_rows, bass.IndirectOffsetOnAxis(ap=place[:, t:t + 1], axis=0),
                            rows[:, t, :], None).then_inc(scattered[g], 16)
            for g in range(GROUPS - 2, GROUPS):
                add_y(g)

            def scatter(i, r, first_half):
                pool.wait_ge(e_y_set[r % 2], first_half)
                pool.wait_ge(dest_set, i + 1)
                pool.sem_inc(scatter_ready, 1)
                nc.gpsimd.indirect_dma_start(
                    expert_rows, bass.IndirectOffsetOnAxis(ap=dest[:, r:r + 1], axis=0),
                    yring[:, r % YRING, :], None, bounds_check=last_row,
                    oob_is_err=False).then_inc(yring_out[r % YRING], 16)

            last_row = pool.to_reg(TOKENS * TOPK - 1)
            with pool.Fori(0, SORTED_TILES // XRING) as k:
                for r in range(XRING):
                    scatter(k * XRING + r, r, k * (XRING // 2) + r // 2 + 1)

            pool.wait_ge(x_again_in, 16 * GROUPS)
            for g in range(GROUPS):
                pool.wait_ge(silu_y_set, g + 1)
                row = rows[:, (g + 1) * GT - 1, 0:C]
                nc.gpsimd.tensor_tensor(row, acc[g % 2][:, GT - 1, :], row, ALU.mult).then_inc(gated_last_set, 1)
                if g < GROUPS - 1:
                    pool.wait_ge(gated_last_set, g + 1)
                    pool.wait_ge(gated_set, g + 1)
                    nc.gpsimd.tensor_tensor(x_of[g], x_of[g], rows[:, g * GT:(g + 1) * GT, 0:C], ALU.add).then_inc(out_set, 1)

        @block.scalar
        def _(act):
            act.dma_start(vec[:], vectors).then_inc(vec_in, 16)
            act.dma_start(bias_sb[:], bias).then_inc(vec_in, 16)
            act.dma_start(router_f[:], router).then_inc(router_in, 16)
            act.sem_inc(down_free, 1)
            act.wait_ge(vec_in, 32)
            nc.scalar.activation(decay[:], vec[:, v_decay, :], ACT.Sigmoid).then_inc(params_set, 1)
            nc.scalar.activation(first[:], vec[:, v_first, :], ACT.Exp).then_inc(params_set, 1)

            def root(n, tiles):
                act.wait_ge(var_eps, n)
                nc.scalar.activation(tmp_b[:, tiles], tmp_a[:, tiles], ACT.Sqrt).then_inc(root_set, 1)

            act.wait_ge(shared_in, 16)
            nc.scalar.copy(wx_hi[:, SHARED], stage[:, SHARED]).then_inc(shared_hi_set, 1)
            root(1, slice(0, TILES // 4))
            def t_hi(g, b):
                act.wait_ge(t_done, g + 1)
                nc.scalar.copy(in_hi[:, b, :], bank[:, 0:2, :]).then_inc(thi_set, 1)

            def keep_rows(g, b):
                act.wait_ge(xn_set, g * GT + GT)
                nc.scalar.copy(rows[:, ds(g * GT, GT), 0:C], x_norm[:, b * GT:(b + 1) * GT, :]).then_inc(rows_kept, 1)

            def set_silu(g):
                act.wait_ge(gate_done, g + 1)
                nc.scalar.activation(silu_g, bank[:, 2, :], ACT.Silu).then_inc(silu_set, 1)

            def expert_hi(e):
                nc.scalar.copy(wx_hi[:, ds(e, 1)], stage[:, ds(e, 1)]).then_inc(experts_hi_set, 1)

            def h_hi(g, b):
                act.wait_ge(h_set, g + 1)
                nc.scalar.copy(mid_hi[:, b, :], h_shared).then_inc(hhi_set, 1)

            def shared_group(g, b, last_=False):
                if not last_:
                    act.wait_ge(logit_done, g)
                    act.wait_ge(up_done, g)
                    t_hi(g + 1, 1 - b)
                keep_rows(g, b)
                act.wait_ge(h_set, g)
                set_silu(g)
                expert_hi(g)
                h_hi(g, b)
                shared_store(g - 1)

            def shared_store(g):
                act.wait_ge(down_done, g + 1)
                act.wait_ge(attn_lo_set, 1)
                nc.scalar.copy(shared_out[:, ds(g * GT * C, GT * C)], bank[:, 5:7, :]).then_inc(down_free, 1)

            t_hi(0, 0)
            keep_rows(0, 0)
            set_silu(0)
            t_hi(1, 1)
            h_hi(0, 0)
            act.wait_ge(attn_in, 16)
            nc.scalar.copy(wa_hi[:], attn_stage).then_inc(attn_hi_set, 1)
            root(2, slice(TILES // 4, TILES))
            act.wait_ge(experts_in, 32)
            expert_hi(0)
            shared_group(1, 1)
            with act.Fori(0, (GROUPS - 4) // 2) as k:
                shared_group(2 * k + 2, 0)
                shared_group(2 * k + 3, 1)
            shared_group(GROUPS - 2, 0)
            root(3, slice(0, TILES))
            shared_group(GROUPS - 1, 1, last_=True)

            act.wait_ge(logit_read, GROUPS)
            act.wait_ge(h_set, GROUPS)
            nc.scalar.activation(route_tmp[1], logit, ACT.Sigmoid).then_inc(score_set, 1)
            shared_store(GROUPS - 1)

            def set_z(g):
                for t in range(GT):
                    nc.scalar.mul(z[:, t, :], rows[:, g * GT + t, 0:C], rstd2[:, ds(g * GT + t, 1)]).then_inc(z_set, 1)

            def set_xt(g, b):
                act.wait_ge(zt_done, g + 1)
                for k in range(KC):
                    nc.scalar.activation(xt[b][:, k, 1:GROUP + 1], bank[:, k, :], ACT.Identity,
                                         bias=vec[:, ln_b, k:k + 1], scale=vec[:, ln_w, k:k + 1]).then_inc(xt_set, 1)

            def k_hi(g):
                act.wait_ge(mix_k_set, 2 * g + 2)
                nc.scalar.copy(in_hi[:, 0, :], mix_k).then_inc(k_hi_set, 1)

            def rwkv_hi(g):
                for k in range(KC):
                    act.wait_ge(rwkv_set, 2 * g + k + 1)
                    nc.scalar.copy(mid_hi[:, k, :], rwkv[:, k * GROUP:(k + 1) * GROUP]).then_inc(rwhi_set, 1)

            def gate_r(g, k):
                act.wait_ge(r_done, 2 * g + k + 1)
                nc.scalar.activation(r_gate[:, k * GROUP:(k + 1) * GROUP], bank[:, 6, :],
                                     ACT.Sigmoid).then_inc(r_set, 1)

            def copy_y(g, pair, first_):
                act.wait_ge(y_done, 2 * g + pair + 1)
                if pair == 0 and not first_:
                    act.wait_ge(s_set, g)
                nc.scalar.copy(y_new[:, pair * GROUP:(pair + 1) * GROUP],
                               bank[:, 7 if pair == 0 else 0, :]).then_inc(y_copied, 1)

            def mix_group(g, b, before_=True, before2=True, after1=True, after2=True):
                if after1 and before_:
                    act.wait_ge(mix_v_set, 2 * g)
                    set_xt(g + 1, 1 - b)
                if before_:
                    rwkv_hi(g - 1)
                if after2:
                    set_z(g + 2)
                gate_r(g, 0)
                if before_:
                    copy_y(g - 1, 0, not before2)
                gate_r(g, 1)
                if after1:
                    act.wait_ge(k_done, g + 1)
                    k_hi(g + 1)
                if before_:
                    copy_y(g - 1, 1, not before2)

            act.wait_ge(rstd2_set, 1)
            act.wait_ge(rows_kept, GROUPS)
            act.wait_ge(experts_lo_set, EXPERTS)
            set_z(0)
            set_xt(0, 0)
            act.wait_ge(zt_done, 1)
            set_z(1)
            act.wait_ge(logit_done, GROUPS)
            k_hi(0)
            set_xt(1, 1)
            mix_group(0, 0, before_=False, before2=False)
            mix_group(1, 1, before2=False)
            with act.Fori(0, (GROUPS - 4) // 2) as k:
                mix_group(2 * k + 2, 0)
                mix_group(2 * k + 3, 1)
            mix_group(GROUPS - 2, 0, after2=False)
            mix_group(GROUPS - 1, 1, after1=False, after2=False)
            rwkv_hi(GROUPS - 1)

            def after(s):
                if s == 0:
                    for pair in range(2):
                        copy_y(GROUPS - 1, pair, False)

            def step(s, u, half, peeled=False):
                def has(d):
                    return not peeled or 0 <= s - d < SORTED_TILES
                if has(0):
                    act.wait_ge(e_t_done, s + 1)
                    if has(2) :
                        act.wait_ge(e_gu_done, s - 1)
                    nc.scalar.copy(in_hi[:, u % 2, 0:C], bank[:, u % 2, 0:C]).then_inc(e_hi_set, 1)
                if has(1):
                    act.wait_ge(e_gu_done, s)
                    if has(3):
                        act.wait_ge(e_h_set, s - 2)
                    nc.scalar.activation(silu_t[:, (u - 1) % 2, :], bank[:, 2 + (u - 1) % 2, 0:INNER],
                                         ACT.Silu).then_inc(e_silu_set, 1)
                if has(2):
                    act.wait_ge(e_ht_done, s - 1)
                    if has(4):
                        act.wait_ge(e_down_done, s - 3)
                    nc.scalar.copy(mid_hi[:, u % 2, 0:INNER], bank[:, 4 + u % 2, 0:INNER]).then_inc(e_hhi_set, 1)
                if has(3) and (u - 3) % 2 == 0:
                    act.wait_ge(e_down_done, s - 2)
                    if has(3 + YRING):
                        act.wait_ge(yring_out[(u - 3) % YRING], 2 * (s - 3 - (u - 3) % YRING))
                    nc.scalar.copy(yring[:, (u - 3) % YRING, :], bank[:, 6, 0:C]).then_inc(e_y_set[0], 1)

            act.wait_ge(v_done, 2 * GROUPS)
            run_steps(act, step, after=after)

            def gate_silu(g, b):
                act.wait_ge(sum_set, g + 1)
                nc.scalar.activation(acc[b], acc[b], ACT.Silu).then_inc(silu_y_set, 1)

            def gate_part(g, b, n, reused):
                act.wait_ge(y_in[g % 6], 16 * (g // 6 + 1))
                if reused:
                    act.wait_ge(gated_set, g - 1)
                    act.wait_ge(gated_last_set, g - 1)
                for t in range(GT):
                    nc.scalar.mul(acc[b][:, t, :], y_slots[b][:, ds(n, 1), t, 0:C].rearrange("p n c -> p (n c)"),
                                  weight1[:, ds(g * GT + t, 1)]).then_inc(part_set, 1)

            gate_part(0, 0, 0, False)
            gate_part(1, 1, 0, False)
            gate_silu(0, 0)
            gate_part(2, 0, 1, True)
            gate_silu(1, 1)
            gate_part(3, 1, 1, True)
            gate_silu(2, 0)
            gate_part(4, 0, 2, True)
            gate_silu(3, 1)
            gate_part(5, 1, 2, True)
            gate_silu(4, 0)
            gate_part(6, 0, 0, True)
            gate_silu(5, 1)
            gate_part(7, 1, 0, True)
            gate_silu(6, 0)
            gate_silu(7, 1)

        def route(dve, link, meanwhile):
            def et(n):
                return route_tmp[n].rearrange("p (e t) -> p e t", e=EXPERTS)

            scores, choice, best = et(1), et(2), et(3)
            half = EXPERTS // 2
            dve.wait_ge(score_set, 1)
            dve.wait_ge(vec_in, 32)
            link(nc.vector.tensor_tensor(choice, scores, bias_sb[:].unsqueeze(2).to_broadcast([P, EXPERTS, TILES]), ALU.add))
            pairs = route_tmp[2].rearrange("p (h a t) -> p h a t", h=EXPERTS // 2, a=2)
            more = route_tmp[4].rearrange("p (h t) -> p h t", h=8)[:, 0:4]
            less = route_tmp[4].rearrange("p (h t) -> p h t", h=8)[:, 4:8]
            link(nc.vector.tensor_tensor(more, pairs[:, :, 0], pairs[:, :, 1], ALU.max))
            link(nc.vector.tensor_tensor(less, pairs[:, :, 0], pairs[:, :, 1], ALU.min))
            more2 = more.rearrange("p (n a) t -> p n a t", n=2)
            less2 = less.rearrange("p (n a) t -> p n a t", n=2)
            w = route_tmp[5].rearrange("p (x n t) -> p x n t", x=4, n=2)
            link(nc.vector.tensor_tensor(w[:, 0], more2[:, :, 0], more2[:, :, 1], ALU.max))
            link(nc.vector.tensor_tensor(w[:, 1], more2[:, :, 0], more2[:, :, 1], ALU.min))
            link(nc.vector.tensor_tensor(w[:, 2], less2[:, :, 0], less2[:, :, 1], ALU.max))
            link(nc.vector.tensor_tensor(w[:, 1], w[:, 1], w[:, 2], ALU.max))
            link(nc.vector.tensor_tensor(w[:, 0], w[:, 0], w[:, 1], ALU.add))
            link(nc.vector.tensor_tensor(w[:, 3, 1], w[:, 0, 1], w[:, 0, 0], ALU.is_gt))
            link(nc.vector.tensor_scalar(w[:, 3, 0], w[:, 3, 1], -1.0, 1.0, ALU.mult, ALU.add))
            for n in range(2):
                part = slice(n * half, (n + 1) * half)
                link(nc.vector.tensor_tensor(best[:, part], choice[:, part],
                                             w[:, 3, n].unsqueeze(1).to_broadcast([P, half, TILES]), ALU.mult))
            dve.wait_ge(table_set, EXPERTS + 2)
            small = route_tmp[7].rearrange("p (x t) -> p x t", x=8)
            is_one, tmp = (et(8), et(9)), et(10)
            for n in range(TOPK):
                top = small[:, 0]
                link(nc.vector.tensor_reduce(top, best.rearrange("p e t -> p t e"), AX.X, ALU.max))
                link(nc.vector.tensor_tensor(tmp, best, top.unsqueeze(1).to_broadcast([P, EXPERTS, TILES]), ALU.is_equal))
                link(nc.vector.tensor_tensor(tmp, tmp, prefer, ALU.mult))
                link(nc.vector.tensor_reduce(top, tmp.rearrange("p e t -> p t e"), AX.X, ALU.max))
                link(nc.vector.tensor_tensor(is_one[n], tmp, top.unsqueeze(1).to_broadcast([P, EXPERTS, TILES]), ALU.is_equal))
                if n == 0:
                    link(nc.vector.scalar_tensor_tensor(best, is_one[0], REMOVED, best, ALU.mult, ALU.add))
            chosen = route_tmp[11].bitcast(BF16)[:, 0:ET]
            nc.vector.tensor_tensor(chosen, route_tmp[8], route_tmp[9], ALU.add).then_inc(chosen_set, 1)
            meanwhile()
            dve.wait_ge(counted, 1)
            within, total = bank[:, 7, 0:ET], bank[:, 7, ET:2 * ET]
            link(nc.vector.tensor_tensor_scan(route_tmp[13], tables[:, 1], total, 0.0, ALU.mult, ALU.add))
            cnt = small[:, 5, 0:EXPERTS]
            tiles = small[:, 6, 0:EXPERTS]
            ends = small[:, 6, EXPERTS:2 * EXPERTS]
            starts = small[:, 6, 2 * EXPERTS:3 * EXPERTS]
            one8 = small[:, 5, EXPERTS:2 * EXPERTS]
            nc.vector.memset(one8, 1.0)
            link(nc.vector.tensor_scalar(int_tmp[:, 0:EXPERTS], et(13)[:, :, TILES - 1], float(P - 1), None, ALU.add))
            link(nc.vector.tensor_scalar(int_tmp[:, 0:EXPERTS], int_tmp[:, 0:EXPERTS], 7, None, ALU.logical_shift_right))
            link(nc.vector.tensor_copy(tiles, int_tmp[:, 0:EXPERTS]))
            link(nc.vector.tensor_tensor_scan(ends, one8, tiles, 0.0, ALU.mult, ALU.add))
            link(nc.vector.tensor_tensor(starts, ends, tiles, ALU.subtract))
            link(nc.vector.tensor_scalar(starts, starts, float(P), None, ALU.mult))
            place = et(13)
            link(nc.vector.tensor_tensor(route_tmp[13], route_tmp[13], total, ALU.subtract))
            link(nc.vector.tensor_tensor(route_tmp[13], within, route_tmp[13], ALU.add))
            link(nc.vector.tensor_tensor(place, place, starts.unsqueeze(2).to_broadcast([P, EXPERTS, TILES]), ALU.add))
            for n, to in enumerate((place1, place2)):
                link(nc.vector.tensor_tensor(tmp, is_one[n], place, ALU.mult))
                link(nc.vector.tensor_reduce(small[:, 1 + n], tmp.rearrange("p e t -> p t e"), AX.X, ALU.add))
                nc.vector.tensor_copy(to[:], small[:, 1 + n]).then_inc(places_set, 1)
            nc.vector.tensor_copy(rows[:, :, C + 1], small[:, 2])
            nc.vector.tensor_scalar(rows[:, :, C], my_place[:, 0:TILES], 2.0, None, ALU.mult).then_inc(places_set, 1)
            column = small[:, 7, EXPERTS:EXPERTS + 1]
            link(nc.vector.tensor_scalar(small[:, 7, 0:EXPERTS], ends, my_place[:, 0:1], None, ALU.is_le))
            link(nc.vector.tensor_reduce(column, small[:, 7, 0:EXPERTS], AX.X, ALU.add))
            nc.vector.tensor_scalar(column, column, float(EXPERTS - 1), float(EW), ALU.min, ALU.mult).then_inc(column_set, 1)

        def route_rest(dve, link):
            dve.wait_ge(column_turned, 1)
            nc.vector.tensor_copy(weight_at[0:1, :], bank[0:1, 7, 0:SORTED_TILES + UNROLL]).then_inc(weight_at_set, 1)
            dve.wait_ge(scores_read, 1)
            inverse = extra[:, 0, 0:TILES]
            link(nc.vector.reciprocal(inverse, chosen_scores[:, 2]))
            nc.vector.tensor_tensor(weight1[:], chosen_scores[:, 0], inverse, ALU.mult)
            nc.vector.tensor_tensor(weight2[:], chosen_scores[:, 1], inverse, ALU.mult)

        @block.vector
        def _(dve):
            steps = [0]

            def link(ins):
                steps[0] += 1
                ins.then_inc(dve_step, 1)
                dve.wait_ge(dve_step, steps[0])

            def statistics(c):
                dve.wait_ge(x_in[c], 16)
                for t in range(c * TILES // 4, (c + 1) * TILES // 4):
                    nc.vector.bn_stats(stats[:, t, :], rows[:, t, 0:C]).then_inc(norm_set, 1)

            def inverse_root(to, tiles, n):
                to, a, b = to[:, tiles], tmp_a[:, tiles], tmp_b[:, tiles]
                dve.wait_ge(root_set, n)
                link(nc.vector.reciprocal(to, b))
                link(nc.vector.tensor_tensor(b, to, to, ALU.mult))
                link(nc.vector.tensor_tensor(b, b, a, ALU.mult))
                link(nc.vector.tensor_scalar(b, b, -0.5, 1.5, ALU.mult, ALU.add))
                link(nc.vector.tensor_tensor(to, to, b, ALU.mult))

            def first_norm(tiles, n):
                dve.wait_ge(norm_set, tiles.stop)
                a, b, part = tmp_a[:, tiles], tmp_b[:, tiles], stats[:, tiles]
                link(nc.vector.tensor_tensor(a, part[:, :, 1], part[:, :, 4], ALU.add))
                link(nc.vector.tensor_scalar(mean[:, tiles], a, 0.5, None, ALU.mult))
                link(nc.vector.tensor_tensor(a, part[:, :, 1], part[:, :, 4], ALU.subtract))
                link(nc.vector.tensor_tensor(a, a, a, ALU.mult))
                link(nc.vector.tensor_scalar(a, a, 0.25, None, ALU.mult))
                link(nc.vector.tensor_tensor(b, part[:, :, 2], part[:, :, 5], ALU.add))
                link(nc.vector.scalar_tensor_tensor(var[:, tiles], b, 1.0 / C, a, ALU.mult, ALU.add))
                nc.vector.tensor_scalar(a, var[:, tiles], LN_EPS, None, ALU.add).then_inc(var_eps, 1)
                inverse_root(rstd, tiles, n)

            def second_norm():
                link(nc.vector.tensor_tensor(tmp_a[:], var[:], rstd[:], ALU.mult))
                link(nc.vector.tensor_tensor(tmp_a[:], tmp_a[:], rstd[:], ALU.mult))
                nc.vector.tensor_scalar(tmp_a[:], tmp_a[:], LN_EPS, None, ALU.add).then_inc(var_eps, 1)
                inverse_root(rstd2, slice(0, TILES), 3)
                dve.sem_inc(rstd2_set, 1)

            def set_xn(g, b, tiles=range(GT), reused=True):
                if reused:
                    dve.wait_ge(t_done, g - 1)
                    dve.wait_ge(rows_kept, g - 1)
                for t in tiles:
                    nc.vector.tensor_scalar(x_norm[:, b * GT + t, :], rows[:, g * GT + t, 0:C],
                                            mean[:, ds(g * GT + t, 1)], rstd[:, ds(g * GT + t, 1)],
                                            ALU.subtract, ALU.mult).then_inc(xn_set, 1)

            def t_lo(g, b):
                dve.wait_ge(thi_set, g + 1)
                nc.vector.tensor_tensor(in_lo[:, b, :], bank[:, 0:2, :].rearrange("p a c -> p (a c)"),
                                        f32(in_hi[:, b, :]), ALU.subtract).then_inc(tlo_set, 1)

            def set_h(g, first_=False):
                dve.wait_ge(silu_set, g + 1)
                dve.wait_ge(up_done, g + 1)
                if not first_:
                    dve.wait_ge(hlo_set, g)
                nc.vector.tensor_tensor(h_shared, bank[:, 3, :], silu_g, ALU.mult).then_inc(h_set, 1)

            def h_lo(g, b, first_=False):
                dve.wait_ge(hhi_set, g + 1)
                if not first_:
                    dve.wait_ge(down_done, g)
                nc.vector.tensor_tensor(mid_lo[:, b, :], h_shared, f32(mid_hi[:, b, :]),
                                        ALU.subtract).then_inc(hlo_set, 1)

            def keep_logits(g, first_=False):
                dve.wait_ge(logit_done, g + 1)
                if not first_:
                    dve.wait_ge(logit_turned, g)
                nc.vector.tensor_copy(logit_rows, bank[0:2 * EXPERTS, 4, :]).then_inc(logit_kept, 1)

            def read_logits(g):
                dve.wait_ge(logit_turned, g + 1)
                parts = bank[:, 7, 0:GT * 2 * EXPERTS].rearrange("p (t h e) -> p h e t", h=2, e=EXPERTS)
                nc.vector.tensor_copy(logit_low, parts[:, 1]).then_inc(logit_low_set, 1)
                dve.wait_ge(logit_low_set, g + 1)
                nc.vector.tensor_tensor(logit.rearrange("p (e t) -> p e t", e=EXPERTS)[:, :, ds(g * GT, GT)],
                                        parts[:, 0], logit_low, ALU.add).then_inc(logit_read, 1)

            def shared_group(g, b, last_=False, xn_ahead=True):
                if not last_:
                    dve.wait_ge(logit_done, g)
                    dve.wait_ge(up_done, g)
                    t_lo(g + 1, 1 - b)
                if xn_ahead:
                    set_xn(g + 2, b, range(0, GT // 2))
                set_h(g)
                keep_logits(g)
                if xn_ahead:
                    set_xn(g + 2, b, range(GT // 2, GT))
                h_lo(g, b)
                read_logits(g)

            statistics(0)
            first_norm(slice(0, TILES // 4), 1)
            set_xn(0, 0, reused=False)
            set_xn(1, 1, reused=False)
            dve.wait_ge(router_in, 16)
            link(nc.vector.tensor_copy(wr[:, :, 0], router_f[:]))
            nc.vector.tensor_tensor(wr[:, :, 1], router_f[:], f32(wr[:, :, 0]), ALU.subtract).then_inc(shared_w_set, 1)
            t_lo(0, 0)
            statistics(1)
            set_h(0, True)
            keep_logits(0, True)
            statistics(2)
            t_lo(1, 1)
            statistics(3)
            first_norm(slice(TILES // 4, TILES), 2)
            set_xn(2, 0)
            h_lo(0, 0, True)
            read_logits(0)
            shared_group(1, 1)
            with dve.Fori(0, (GROUPS - 4) // 2) as k:
                shared_group(2 * k + 2, 0)
                shared_group(2 * k + 3, 1)
            shared_group(GROUPS - 2, 0, xn_ahead=False)
            second_norm()
            shared_group(GROUPS - 1, 1, last_=True, xn_ahead=False)

            def mixture(to, done, which, g, b):
                for k in range(KC):
                    cols = slice(k * GROUP, (k + 1) * GROUP)
                    nc.vector.scalar_tensor_tensor(to[:, cols], diff[b][:, cols], vec[:, which, k:k + 1],
                                                   xt[b][:, k, 0:GROUP], ALU.mult, ALU.add).then_inc(done, 1)

            def k_lo(g):
                dve.wait_ge(k_hi_set, g + 1)
                nc.vector.tensor_tensor(in_lo[:, 0, :], mix_k, f32(in_hi[:, 0, :]),
                                        ALU.subtract).then_inc(k_lo_set, 1)

            dve.wait_ge(experts_lo_set, EXPERTS)
            nc.vector.memset(xt[0][:, :, 0:1], 0.0).then_inc(edge_zero, 1)
            def first_mixtures():
                dve.wait_ge(params_set, 2)
                dve.wait_ge(diff_set, 1)
                mixture(mix_k, mix_k_set, mk, 0, 0)
                mixture(mix_r, mix_r_set, mr, 0, 0)
                k_lo(0)

            route(dve, link, first_mixtures)

            def finish_rwkv(g):
                for k in range(KC):
                    dve.wait_ge(k_read, 2 * g + k + 1)
                    dve.wait_ge(v_done, 2 * g + k + 1)
                    cols = slice(k * GROUP, (k + 1) * GROUP)
                    nc.vector.tensor_tensor(rwkv[:, cols], rwkv[:, cols], bank[:, 4 + k, :],
                                            ALU.mult).then_inc(v_read, 1)
                for k in range(KC):
                    dve.wait_ge(v_read, 2 * g + k + 1)
                    dve.wait_ge(r_set, 2 * g + k + 1)
                    cols = slice(k * GROUP, (k + 1) * GROUP)
                    nc.vector.tensor_tensor(rwkv[:, cols], rwkv[:, cols], r_gate[:, cols],
                                            ALU.mult).then_inc(rwkv_set, 1)
                for k in range(KC):
                    dve.wait_ge(rwhi_set, 2 * g + k + 1)
                    nc.vector.tensor_tensor(mid_lo[:, k, :], rwkv[:, k * GROUP:(k + 1) * GROUP],
                                            f32(mid_hi[:, k, :]), ALU.subtract).then_inc(rwlo_set, 1)

            def scan(g, b, before_):
                if before_:
                    dve.wait_ge(rwlo_set, 2 * g)
                dve.wait_ge(k_done, g + 1)
                for k in range(KC):
                    cols = slice(k * GROUP, (k + 1) * GROUP)
                    nc.vector.tensor_tensor_scan(rwkv[:, cols], decay[:, k:k + 1].to_broadcast([P, GROUP]),
                                                 bank[:, 2 + k, :], 0.0 if b == 0 else last_s[:, k:k + 1],
                                                 ALU.mult, ALU.add).then_inc(scan_set, 1)
                dve.wait_ge(scan_set, 2 * g + 2)
                nc.vector.tensor_copy(last_s[:], rwkv.rearrange("p (k t) -> p k t", k=KC)[:, :, GROUP - 1]).then_inc(last_set, 1)
                dve.wait_ge(last_set, g + 1)
                for k in range(KC):
                    cols = slice(k * GROUP, (k + 1) * GROUP)
                    nc.vector.scalar_tensor_tensor(rwkv[:, cols], rwkv[:, cols], first[:, k:k + 1],
                                                   bank[:, 2 + k, :], ALU.mult, ALU.add).then_inc(k_read, 1)

            def mix_group(g, b, before_=True, after1=True):
                if before_:
                    finish_rwkv(g - 1)
                scan(g, b, before_)
                mixture(mix_v, mix_v_set, mv, g, b)
                if after1:
                    dve.wait_ge(diff_set, g + 2)
                    mixture(mix_k, mix_k_set, mk, g + 1, 1 - b)
                    dve.wait_ge(r_done, 2 * g + 2)
                    mixture(mix_r, mix_r_set, mr, g + 1, 1 - b)
                    k_lo(g + 1)

            mix_group(0, 0, before_=False)
            route_rest(dve, link)
            with dve.Fori(0, (GROUPS - 2) // 2) as k:
                mix_group(2 * k + 1, 1)
                mix_group(2 * k + 2, 0)
            mix_group(GROUPS - 1, 1, after1=False)
            finish_rwkv(GROUPS - 1)

            def step(s, u, half, peeled=False):
                def has(d):
                    return not peeled or 0 <= s - d < SORTED_TILES
                if has(0):
                    dve.wait_ge(e_hi_set, s + 1)
                    nc.vector.tensor_tensor(in_lo[:, u % 2, 0:C], bank[:, u % 2, 0:C], f32(in_hi[:, u % 2, 0:C]),
                                            ALU.subtract).then_inc(e_lo_set, 1)
                if has(1):
                    dve.wait_ge(e_silu_set, s)
                    if has(3):
                        dve.wait_ge(e_ht_done, s - 2)
                    nc.vector.tensor_tensor(h_t[:, (u - 1) % 2, :], bank[:, 2 + (u - 1) % 2, INNER:2 * INNER],
                                            silu_t[:, (u - 1) % 2, :], ALU.mult).then_inc(e_h_set, 1)
                if has(2):
                    dve.wait_ge(e_hhi_set, s - 1)
                    nc.vector.tensor_tensor(mid_lo[:, u % 2, 0:INNER], bank[:, 4 + u % 2, 0:INNER],
                                            f32(mid_hi[:, u % 2, 0:INNER]), ALU.subtract).then_inc(e_hlo_set, 1)
                if has(3):
                    slot = (u - 3) % XRING
                    dve.wait_ge(xring_in[slot], 2 * (s - 3) + 16 - 2 * slot)
                    if has(3 + XRING):
                        dve.wait_ge(yring_out[slot], 2 * (s - 3 - slot))
                    nc.vector.scalar_tensor_tensor(dest[:, slot:slot + 1], xring[:, slot, C + 1:C + 2],
                                                   my_place[:, ds(s - 3, 1)], xring[:, slot, C:C + 1],
                                                   ALU.is_equal, ALU.add).then_inc(dest_set, 1)
                if has(3) and (u - 3) % 2 == 1:
                    dve.wait_ge(e_down_done, s - 2)
                    nc.vector.tensor_copy(yring[:, (u - 3) % YRING, :], bank[:, 7, 0:C]).then_inc(e_y_set[1], 1)

            run_steps(dve, step)

            def gate_sum(g, b, n):
                for t in range(GT):
                    dve.wait_ge(part_set, g * GT + t + 1)
                    nc.vector.scalar_tensor_tensor(acc[b][:, t, :], y_slots[b][:, n, t, C:2 * C],
                                                   weight2[:, g * GT + t:g * GT + t + 1], acc[b][:, t, :],
                                                   ALU.mult, ALU.add).then_inc(routed_set, 1)

            def gate_add_shared(g, b):
                dve.wait_ge(routed_set, g * GT + GT)
                flat = acc[b].rearrange("p t c -> p (t c)")
                nc.vector.tensor_tensor(flat, flat, shared_out[:, g * GT * C:(g + 1) * GT * C], ALU.add).then_inc(sum_set, 1)

            def gate_product(g, b):
                dve.wait_ge(silu_y_set, g + 1)
                row = rows[:, g * GT:(g + 1) * GT - 1, 0:C]
                nc.vector.tensor_tensor(row, acc[b][:, 0:GT - 1], row, ALU.mult).then_inc(gated_set, 1)

            dve.wait_ge(s_set, GROUPS)
            for g in range(GROUPS):
                gate_sum(g, g % 2, g // 2 % 3)
                if g >= 1:
                    gate_product(g - 1, (g - 1) % 2)
                gate_add_shared(g, g % 2)
            gate_product(GROUPS - 1, 1)
            dve.wait_ge(x_again_in, 16 * GROUPS)
            dve.wait_ge(gated_set, GROUPS)
            dve.wait_ge(gated_last_set, GROUPS)
            to = x_of[GROUPS - 1]
            nc.vector.tensor_tensor(to, to, rows[:, TILES - GT:TILES, 0:C], ALU.add).then_inc(last_out_set, 1)

        @block.tensor
        def _(pe):
            pe.wait_ge(const_set, 5)

            def product(out_ap, hi_l, lo_l, hi_r, lo_r, first_, last_, lolo=False):
                nc.tensor.matmul(out_ap, hi_l, hi_r, start=first_, stop=False)
                nc.tensor.matmul(out_ap, hi_l, lo_r, start=False, stop=False)
                if lolo:
                    nc.tensor.matmul(out_ap, lo_l, lo_r, start=False, stop=False)
                return nc.tensor.matmul(out_ap, lo_l, hi_r, start=False, stop=last_)

            def transposes(g, b):
                pe.wait_ge(xn_set, GT * (g + 1))
                for k in range(KC):
                    for t in range(GT):
                        mm = nc.tensor.transpose(bank[:, k, t * P:(t + 1) * P],
                                                 x_norm[:, b * GT + t, k * P:(k + 1) * P], ident[:])
                mm.then_inc(t_done, 1)

            def gate_up(g, b):
                pe.wait_ge(thi_set, g + 1)
                pe.wait_ge(tlo_set, g + 1)
                for n, done in ((0, gate_done), (1, up_done)):
                    for k in range(KC):
                        cols = slice((2 * k + n) * INNER, (2 * k + n + 1) * INNER)
                        tok = slice(k * GROUP, (k + 1) * GROUP)
                        mm = product(bank[:, 2 + n, :], wx_hi[:, SHARED, cols], wx_lo[:, SHARED, cols],
                                     in_hi[:, b, tok], in_lo[:, b, tok], k == 0, k == KC - 1)
                    mm.then_inc(done, 1)

            def down(g, b):
                pe.wait_ge(hhi_set, g + 1)
                pe.wait_ge(hlo_set, g + 1)
                pe.wait_ge(down_free, g + 1)
                for t in range(GT):
                    tok = slice(t * P, (t + 1) * P)
                    mm = product(bank[:, 5 + t // 2, (t % 2) * C:(t % 2 + 1) * C],
                                 mid_hi[:, b, tok], mid_lo[:, b, tok],
                                 wx_hi[:, SHARED, EW - C:EW], wx_lo[:, SHARED, EW - C:EW], True, True)
                mm.then_inc(down_done, 1)

            def logits(g, b, first_=False):
                if not first_:
                    pe.wait_ge(logit_kept, g)
                both = [wr[:, k].rearrange("p h e -> p (h e)") for k in range(KC)]
                for k in range(KC):
                    tok = slice(k * GROUP, (k + 1) * GROUP)
                    nc.tensor.matmul(bank[0:2 * EXPERTS, 4, :], both[k], in_hi[:, b, tok], start=k == 0, stop=False)
                    mm = nc.tensor.matmul(bank[0:2 * EXPERTS, 4, :], both[k], in_lo[:, b, tok],
                                          start=False, stop=k == KC - 1)
                mm.then_inc(logit_done, 1)

            def turn_logits(g, first_=False):
                pe.wait_ge(logit_kept, g + 1)
                if not first_:
                    pe.wait_ge(logit_read, g)
                pe.sem_inc(turn_ready, 1)
                for t in range(GT):
                    mm = nc.tensor.transpose(bank[:, 7, t * 2 * EXPERTS:(t + 1) * 2 * EXPERTS],
                                             logit_rows[:, t * P:(t + 1) * P], ident[0:2 * EXPERTS, 0:2 * EXPERTS])
                mm.then_inc(logit_turned, 1)

            def next_transposes(g, b):
                pe.wait_ge(thi_set, g + 1)
                pe.wait_ge(tlo_set, g + 1)
                transposes(g + 1, 1 - b)

            def next_gate_up(g, b):
                pe.wait_ge(silu_set, g)
                pe.wait_ge(h_set, g)
                gate_up(g, b)

            def shared_group(g, b, last_=False):
                if not last_:
                    next_transposes(g, b)
                next_gate_up(g, b)
                logits(g, b)
                down(g - 1, 1 - b)
                turn_logits(g)

            transposes(0, 0)
            pe.wait_ge(shared_w_set, 2)
            gate_up(0, 0)
            logits(0, 0, True)
            next_transposes(0, 0)
            turn_logits(0, True)
            next_gate_up(1, 1)
            next_transposes(1, 1)
            logits(1, 1)
            down(0, 0)
            turn_logits(1)
            with pe.Fori(0, (GROUPS - 4) // 2) as k:
                shared_group(2 * k + 2, 0)
                shared_group(2 * k + 3, 1)
            shared_group(GROUPS - 2, 0)
            shared_group(GROUPS - 1, 1, last_=True)
            down(GROUPS - 1, 1)

            def z_transposes(g):
                pe.wait_ge(z_set, GT * (g + 1))
                for k in range(KC):
                    for t in range(GT):
                        mm = nc.tensor.transpose(bank[:, k, t * P:(t + 1) * P], z[:, t, k * P:(k + 1) * P], ident[:])
                mm.then_inc(zt_done, 1)

            z_transposes(0)

            pe.wait_ge(chosen_set, 1)
            chosen = route_tmp[11].bitcast(BF16)[:, 0:ET]
            nc.tensor.matmul(bank[:, 7, 0:ET], before[:], chosen, start=True, stop=True)
            nc.tensor.matmul(bank[:, 7, ET:2 * ET], ones[:], chosen, start=True, stop=True).then_inc(counted, 1)

            def project_k(d):
                for k in range(KC):
                    cols = slice(d * P, (d + 1) * P)
                    tok = slice(k * GROUP, (k + 1) * GROUP)
                    mm = product(bank[:, 2 + d, :], wa_hi[:, 0, k, cols], wa_lo[:, 0, k, cols],
                                 in_hi[:, 0, tok], in_lo[:, 0, tok], k == 0, k == KC - 1)
                return mm

            def project(w, d, bank_no, mixed):
                for k in range(KC):
                    mm = nc.tensor.matmul(bank[:, bank_no, :], wa[:, w, k, d * P:(d + 1) * P],
                                          mixed[:, k * GROUP:(k + 1) * GROUP], start=k == 0, stop=k == KC - 1)
                return mm

            def y_out(g, pair):
                for t in range(2):
                    for k in range(KC):
                        tok = slice((2 * pair + t) * P, (2 * pair + t + 1) * P)
                        mm = product(bank[:, 7 if pair == 0 else 0, t * C:(t + 1) * C],
                                     mid_hi[:, k, tok], mid_lo[:, k, tok],
                                     wa_hi[:, 1, k, :], wa_lo[:, 1, k, :], k == 0, k == KC - 1)
                mm.then_inc(y_done, 1)

            def mix_group(g, b, before_=True, before2=True, after1=True):
                if before2:
                    pe.wait_ge(y_copied, 2 * g - 2)
                if after1:
                    pe.wait_ge(xt_set, 2 * g + 2)
                    z_transposes(g + 1)
                pe.wait_ge(k_hi_set, g + 1)
                pe.wait_ge(k_lo_set, g + 1)
                if before_:
                    pe.wait_ge(k_read, 2 * g)
                for d in range(KC):
                    mm = project_k(d)
                mm.then_inc(k_done, 1)
                for d in range(KC):
                    pe.wait_ge(mix_r_set, 2 * g + 2)
                    if d == 1 or before_:
                        pe.wait_ge(r_set, 2 * g + d)
                    project(0, d, 6, mix_r).then_inc(r_done, 1)
                    if before_:
                        if d == 0:
                            pe.wait_ge(rwhi_set, 2 * g)
                            pe.wait_ge(rwlo_set, 2 * g)
                        elif after1:
                            pe.wait_ge(xt_set, 2 * g + 4)
                        y_out(g - 1, d)
                if not before_:
                    pe.wait_ge(column_set, 1)
                    nc.tensor.transpose(bank[0:1, 7, 0:P], route_tmp[7][:, 7 * TILES + EXPERTS:7 * TILES + EXPERTS + 1],
                                        ident[:]).then_inc(column_turned, 1)
                pe.wait_ge(mix_v_set, 2 * g + 2)
                if before_:
                    pe.wait_ge(v_read, 2 * g)
                for d in range(KC):
                    project(1, d, 4 + d, mix_v).then_inc(v_done, 1)

            pe.wait_ge(attn_lo_set, 1)
            pe.wait_ge(wa_in, 16)
            pe.wait_ge(logit_read, GROUPS)
            pe.wait_ge(down_free, GROUPS + 1)
            mix_group(0, 0, before_=False, before2=False)
            mix_group(1, 1, before2=False)
            with pe.Fori(0, (GROUPS - 4) // 2) as k:
                mix_group(2 * k + 2, 0)
                mix_group(2 * k + 3, 1)
            mix_group(GROUPS - 2, 0)
            mix_group(GROUPS - 1, 1, after1=False)
            pe.wait_ge(y_copied, 2 * GROUPS - 2)

            def after(s):
                if s == 0:
                    pe.wait_ge(rwhi_set, 2 * GROUPS)
                    pe.wait_ge(rwlo_set, 2 * GROUPS)
                    y_out(GROUPS - 1, 0)
                    pe.wait_ge(e_lo_set, 1)
                    y_out(GROUPS - 1, 1)
                elif s == 1:
                    pe.wait_ge(y_copied, 2 * GROUPS)

            pe.wait_ge(weight_at_set, 1)
            pe.wait_ge(experts_lo_set, EXPERTS)

            wx_hi_flat = wx_hi[:].rearrange("p e w -> p (e w)")
            wx_lo_flat = wx_lo[:].rearrange("p e w -> p (e w)")

            tile_regs = [pe.alloc_register(f"weights_of_{j}") for j in range(UNROLL + 2)]
            weights_of = {}

            def load_weights(tile, n):
                pe.load(tile_regs[0:n], weight_at[0:1, ds(tile, n)])

            def use_weights(first_key, n):
                weights_of.clear()
                for j in range(n):
                    weights_of[first_key + j] = pe.snap(tile_regs[j], min_val=0, max_val=(EXPERTS - 1) * EW)

            def step(s, u, half, peeled=False):
                def has(d):
                    return not peeled or 0 <= s - d < SORTED_TILES
                if has(0):
                    slot = u % XRING
                    pe.wait_ge(xring_in[slot], 2 * s + 16 - 2 * slot)
                    if has(2):
                        pe.wait_ge(e_lo_set, s - 1)
                    for k in range(KC):
                        mm = nc.tensor.transpose(bank[:, u % 2, k * P:(k + 1) * P],
                                                 xring[:, slot, k * P:(k + 1) * P], ident[:])
                    mm.then_inc(e_t_done, 1)
                if has(1):
                    v = weights_of[u - 1]
                    pe.wait_ge(e_lo_set, s)
                    if has(3):
                        pe.wait_ge(e_h_set, s - 2)
                    b = (u - 1) % 2
                    for k in range(KC):
                        tok = slice(k * P, (k + 1) * P)
                        mm = product(bank[:, 2 + b, 0:2 * INNER], in_hi[:, b, tok], in_lo[:, b, tok],
                                     wx_hi_flat[:, ds(v + k * 2 * INNER, 2 * INNER)],
                                     wx_lo_flat[:, ds(v + k * 2 * INNER, 2 * INNER)], k == 0, k == KC - 1)
                    mm.then_inc(e_gu_done, 1)
                    if (u + 1 - HEAD) % UNROLL == 0:
                        load_weights(s - 2, UNROLL + 2)
                if has(2):
                    pe.wait_ge(e_h_set, s - 1)
                    if has(4):
                        pe.wait_ge(e_hlo_set, s - 3)
                    nc.tensor.transpose(bank[:, 4 + u % 2, 0:P], h_t[:, u % 2, :], ident[:]).then_inc(e_ht_done, 1)
                if has(3):
                    v = weights_of[u - 3]
                    pe.wait_ge(e_hlo_set, s - 2)
                    b = (u - 3) % 2
                    if has(5):
                        pe.wait_ge(e_y_set[b], half)
                    product(bank[:, 6 + b, 0:C], mid_hi[:, b, 0:INNER], mid_lo[:, b, 0:INNER],
                            wx_hi_flat[:, ds(v + 2 * KC * INNER, C)],
                            wx_lo_flat[:, ds(v + 2 * KC * INNER, C)], True, True).then_inc(e_down_done, 1)

            load_weights(0, HEAD - 1)
            run_steps(pe, step, use_weights, after)


def kernel(**inputs):
    import numpy as np
    import concourse.bacc as bacc
    from concourse.bass_utils import run_bass_kernel_spmd

    given = {name.removeprefix("L0_"): np.asarray(a) for name, a in inputs.items()}

    def chunks(a):
        return a.reshape(KC, P, -1).transpose(1, 0, 2)

    vectors = np.stack([given["attn_" + n].reshape(KC, P).T for n in
                        ("time_mix_k", "time_mix_v", "time_mix_r", "time_decay", "time_first", "ln_w", "ln_b")], 1)
    experts = [np.concatenate([given["ffn_w_" + n], given["ffn_sw_" + n][None]]) for n in ("gate", "up", "down")]
    gate_up = np.stack([w.reshape(EXPERTS + 1, KC, P, INNER) for w in experts[0:2]], 3).transpose(2, 0, 1, 3, 4)
    arrays = {
        "x": given["attn_x"],
        "vectors": vectors,
        "bias": np.broadcast_to(given["ffn_correction_bias"], (P, EXPERTS)),
        "router": chunks(given["ffn_router_weight"].T),
        "wk_wo": np.stack([chunks(given["attn_" + n].T) for n in ("Wk", "Wo")], 1),
        "wr_wv": np.stack([chunks(given["attn_" + n].T) for n in ("Wr", "Wv")], 1),
        "expert_w": np.concatenate([gate_up.reshape(P, EXPERTS + 1, -1), experts[2].transpose(1, 0, 2)], 2),
    }
    arrays = {name: np.ascontiguousarray(a) for name, a in arrays.items()}
    nc = bacc.Bacc("TRN2", target_bir_lowering=False, num_devices=1)
    args = [nc.dram_tensor(name, a.shape, F32, kind="ExternalInput").ap() for name, a in arrays.items()]
    out = nc.dram_tensor("out", (BATCH, SEQ, C), F32, kind="ExternalOutput").ap()
    gated_time_mix_kernel(nc, *args, out)
    result = run_bass_kernel_spmd(nc, [arrays], core_ids=[0])
    return result.results[0]["out"]
```
